# Optimizing a Trainium2 kernel written in Bass

```python
import numpy as np
import jax
import jax.numpy as jnp

def _softmax(x, axis=-1):
    return jax.nn.softmax(x, axis=axis)

def _gelu(x):
    return jax.nn.gelu(x, approximate=True)

def _silu(x):
    return jax.nn.silu(x)

def _sigmoid(x):
    return jax.nn.sigmoid(x)

def _layernorm(x, axis=-1, eps=1e-05):
    m = jnp.mean(x, axis=axis, keepdims=True)
    v = jnp.var(x, axis=axis, keepdims=True)
    return (x - m) / jnp.sqrt(v + eps)

def _scatter_add(tgt, idx, src, axis=0):
    return tgt.at[idx].add(src)

def _segment_sum(src, seg, n):
    return jax.ops.segment_sum(src, seg, n)
kernel_name = 'mk_flamingo_gated_d1_seqx_r8_d6c229'

def setup_inputs(seed: int=0):
    np.random.seed(seed)
    _w = jnp.asarray

    def _rec_inputs():
        import jax
        import jax.numpy as jnp
        _rk = jax.random.key(seed)
        x = -7.109e-05 + 0.9999 * jax.random.normal(jax.random.fold_in(_rk, 1), (4, 256, 256), jnp.float32)
        _lenS = 256 - jax.random.randint(jax.random.fold_in(_rk, 7), (4,), 0, max(1, 256 // 4) + 1, jnp.int32)
        _lenS2 = 256 - jax.random.randint(jax.random.fold_in(_rk, 8), (4,), 0, max(1, 256 // 4) + 1, jnp.int32)
        _ctx_2048P = jax.random.normal(jax.random.fold_in(_rk, 11), (4, 16, 256), jnp.float32)
        _ctx_2048c = jax.random.dirichlet(jax.random.fold_in(_rk, 511), 0.3 * jnp.ones((16,), jnp.float32), (4, 256))
        _ctx_2048t = jnp.einsum('bsk,bkd->bsd', _ctx_2048c, _ctx_2048P)
        _ctx_2048t = _ctx_2048t * jax.lax.rsqrt(jnp.mean(jnp.square(_ctx_2048t)) + 1e-12) * 0.953939
        ctx_2048 = -3.05549e-07 + 0.0199987 * (_ctx_2048t + 0.3 * jax.random.normal(jax.random.fold_in(_rk, 611), (4, 256, 256), jnp.float32))
        _g = jax.random.normal(jax.random.fold_in(_rk, 9001), (2, 1), jnp.float32)
        _g = jnp.sign(_g) * jnp.maximum(jnp.abs(_g), 1.0) + (_g == 0) * 1.0
        g_xattn = _g[0]
        g_ffn = _g[1]
        return (x, ctx_2048, g_xattn, g_ffn)
    x, ctx_2048, g_xattn, g_ffn = _rec_inputs()

    def _L0_xattn_setup():
        import jax, jax.numpy as jnp
        import numpy as np
        FP8_MAX = 448.0
        ACT_EPS = 0.0001
        W_EPS = 1e-06
        BLK = 128

        def quant_dequant_act_1x128(x):
            E, M, K = x.shape
            xb = x.reshape(E, M, K // BLK, BLK)
            amax = jnp.max(jnp.abs(xb), axis=-1, keepdims=True)
            safe = jnp.maximum(amax, ACT_EPS)
            q = (xb * (FP8_MAX / safe)).astype(jnp.float8_e4m3fn)
            return (q.astype(jnp.float32) * (safe / FP8_MAX)).reshape(E, M, K)

        def quant_dequant_weight_128x128(w):
            E, N, K = w.shape
            wb = w.reshape(E, N // BLK, BLK, K // BLK, BLK)
            amax = jnp.max(jnp.abs(wb), axis=(2, 4), keepdims=True)
            safe = jnp.maximum(amax, W_EPS)
            q = (wb * (FP8_MAX / safe)).astype(jnp.float8_e4m3fn)
            return (q.astype(jnp.float32) * (safe / FP8_MAX)).reshape(E, N, K)
        key = jax.random.key(seed)
        kx, kw = jax.random.split(key)
        E, M, K, N = (8, 512, 256, 256)
        x = jax.random.normal(kx, (E, M, K), dtype=jnp.float32)
        weight = jax.random.normal(kw, (E, N, K), dtype=jnp.float32) * 0.02
        return {'x': x, 'weight': weight}
    _L0_xattn_all = _L0_xattn_setup()
    _L0_xattn_in = {k: v for k, v in _L0_xattn_all.items() if k in ()}
    del _L0_xattn_all

    def _L0_ffn_setup():
        import jax, jax.numpy as jnp
        import numpy as np
        B, S, H = (1, 128, 256)
        E, K = (8, 4)
        I = 176
        IS = 704
        key = jax.random.key(seed)
        ks = jax.random.split(key, 9)
        s = 0.02
        return {'hidden_states': jax.random.normal(ks[0], (B, S, H), jnp.float32), 'gate_w': jax.random.normal(ks[1], (E, H), jnp.float32) * s, 'shared_gate_w': jax.random.normal(ks[2], (1, H), jnp.float32) * s, 'wg': jax.random.normal(ks[3], (E, I, H), jnp.float32) * s, 'wu': jax.random.normal(ks[4], (E, I, H), jnp.float32) * s, 'wd': jax.random.normal(ks[5], (E, H, I), jnp.float32) * s, 'swg': jax.random.normal(ks[6], (IS, H), jnp.float32) * s, 'swu': jax.random.normal(ks[7], (IS, H), jnp.float32) * s, 'swd': jax.random.normal(ks[8], (H, IS), jnp.float32) * s}
    _L0_ffn_all = _L0_ffn_setup()
    _L0_ffn_in = {k: v for k, v in _L0_ffn_all.items() if k in ('gate_w', 'shared_gate_w', 'wg', 'wu', 'wd', 'swg', 'swu', 'swd')}
    del _L0_ffn_all
    return {'x': x, 'ctx_2048': ctx_2048, 'g_xattn': g_xattn, 'g_ffn': g_ffn, 'L0_ffn_gate_w': _L0_ffn_in['gate_w'], 'L0_ffn_shared_gate_w': _L0_ffn_in['shared_gate_w'], 'L0_ffn_wg': _L0_ffn_in['wg'], 'L0_ffn_wu': _L0_ffn_in['wu'], 'L0_ffn_wd': _L0_ffn_in['wd'], 'L0_ffn_swg': _L0_ffn_in['swg'], 'L0_ffn_swu': _L0_ffn_in['swu'], 'L0_ffn_swd': _L0_ffn_in['swd']}

def reference(x, ctx_2048, g_xattn, g_ffn, L0_ffn_gate_w, L0_ffn_shared_gate_w, L0_ffn_wg, L0_ffn_wu, L0_ffn_wd, L0_ffn_swg, L0_ffn_swu, L0_ffn_swd):
    import jax
    import jax.numpy as jnp

    def _L0_xattn_ref(x, weight):
        import jax, jax.numpy as jnp
        import numpy as np
        FP8_MAX = 448.0
        ACT_EPS = 0.0001
        W_EPS = 1e-06
        BLK = 128

        def quant_dequant_act_1x128(x):
            E, M, K = x.shape
            xb = x.reshape(E, M, K // BLK, BLK)
            amax = jnp.max(jnp.abs(xb), axis=-1, keepdims=True)
            safe = jnp.maximum(amax, ACT_EPS)
            q = (xb * (FP8_MAX / safe)).astype(jnp.float8_e4m3fn)
            return (q.astype(jnp.float32) * (safe / FP8_MAX)).reshape(E, M, K)

        def quant_dequant_weight_128x128(w):
            E, N, K = w.shape
            wb = w.reshape(E, N // BLK, BLK, K // BLK, BLK)
            amax = jnp.max(jnp.abs(wb), axis=(2, 4), keepdims=True)
            safe = jnp.maximum(amax, W_EPS)
            q = (wb * (FP8_MAX / safe)).astype(jnp.float8_e4m3fn)
            return (q.astype(jnp.float32) * (safe / FP8_MAX)).reshape(E, N, K)
        xq = quant_dequant_act_1x128(x)
        wq = quant_dequant_weight_128x128(weight)
        return jnp.einsum('emk,enk->emn', xq, wq)

    def _L0_ffn_ref(hidden_states, gate_w, shared_gate_w, wg, wu, wd, swg, swu, swd):
        import jax, jax.numpy as jnp
        import numpy as np
        B, S, H = (1, 128, 256)
        E, K = (8, 4)
        I = 176
        IS = 704
        b, s, h = hidden_states.shape
        x = hidden_states.reshape(-1, h)
        T = x.shape[0]
        logits = x @ gate_w.T
        probs = jax.nn.softmax(logits.astype(jnp.float32), axis=-1)
        top_w, top_i = jax.lax.top_k(probs, K)
        top_w = top_w / jnp.sum(top_w, axis=-1, keepdims=True)
        top_w = top_w.astype(x.dtype)
        comb = jnp.zeros((T, gate_w.shape[0]), x.dtype)
        comb = comb.at[jnp.arange(T)[:, None], top_i].add(top_w)
        g = jnp.einsum('th,eih->eti', x, wg)
        u = jnp.einsum('th,eih->eti', x, wu)
        y = jnp.einsum('eti,ehi->eth', jax.nn.silu(g) * u, wd)
        moe_out = jnp.einsum('te,eth->th', comb, y)
        sh = jax.nn.silu(x @ swg.T) * (x @ swu.T) @ swd.T
        sgate = jax.nn.sigmoid(x @ shared_gate_w.T)
        out = moe_out + sgate * sh
        return out.reshape(b, s, h)
    x = x + jnp.tanh(g_xattn[0]) * _L0_xattn_ref(_layernorm(x, axis=-1), ctx_2048)
    x = x + jnp.tanh(g_ffn[0]) * _L0_ffn_ref(_layernorm(x, axis=-1), L0_ffn_gate_w, L0_ffn_shared_gate_w, L0_ffn_wg, L0_ffn_wu, L0_ffn_wd, L0_ffn_swg, L0_ffn_swu, L0_ffn_swd)
    return x

_drawn_inputs = setup_inputs


def setup_inputs(seed=0):
    import zlib

    import numpy as np

    out = dict(_drawn_inputs(seed))
    spreads = {}
    factors = {'L0_ffn_gate_w': 8.0,
     'L0_ffn_shared_gate_w': 8.0,
     'L0_ffn_wg': 8.0,
     'L0_ffn_wu': 8.0,
     'L0_ffn_wd': 8.0,
     'L0_ffn_swg': 4.434,
     'L0_ffn_swu': 4.376,
     'L0_ffn_swd': 4.357}
    for name, (base, spread) in spreads.items():
        noise = np.random.default_rng([zlib.crc32(name.encode()), seed]).standard_normal(out[name].shape)
        drawn = base * np.exp(spread * noise) if base else spread * noise
        out[name] = jnp.asarray(drawn.astype(out[name].dtype))
    for name, factor in factors.items():
        out[name] = (out[name] * factor).astype(out[name].dtype)
    return out
```

```python
from contextlib import ExitStack

import concourse.bass as bass
from concourse import mybir

P = 128
B, S, D = 4, 256, 256
T = B * S
TILES = T // P
HALVES = 2
HT = TILES // HALVES
HN = HT * P
HB = B // HALVES
KC = D // P
E, TOP = 8, 4
EI, SI = 176, 704
ROWS = E * EI + SI
FULL = ROWS // P
LAST = ROWS - FULL * P
UNITS = FULL + 1
G = E + 1
GP = G + 1
GU = 2 * KC * P
WC = GU + D
GUL = KC * P
LN_EPS = 1e-5
FP8_MAX, ACT_EPS, W_EPS = 448.0, 1e-4, 1e-6
EXP_BITS = 0x7F800000
SUBNORMAL = 2.0 ** -6
MAGIC = 1.5 * 2.0 ** 20

F32, F32R = mybir.dt.float32, mybir.dt.float32r
BF16, F16, I32 = mybir.dt.bfloat16, mybir.dt.float16, mybir.dt.int32
ALU = mybir.AluOpType
ACT = mybir.ActivationFunctionType
AX = mybir.AxisListType


def flamingo_gated_block(nc, xs, ctx_t, g_x, g_f, gate_t, w_full, w_last, sel, out_t):
    with ExitStack() as stack:
        def sb(name, shape, dt=F32):
            return stack.enter_context(nc.sbuf_tensor(name, shape, dt))

        def sem(name):
            return stack.enter_context(nc.semaphore(name))

        x = sb("x", [P, TILES, D])
        xc = sb("xc", [P, TILES, KC, P])
        xe = sb("xe", [P, TILES, KC, P])
        xq = sb("xq", [P, TILES, KC, P], BF16)
        xqt = sb("xqt", [P, HALVES, KC, HN], BF16)
        cw = sb("cw", [P, B, KC, 2, P])
        ce = sb("ce", [P, B, KC, 2, P])
        cq = sb("cq", [P, B, KC, 2 * P], BF16)
        x1 = sb("x1", [P, TILES, D])
        y2 = sb("y2", [P, TILES, D])
        x1t = sb("x1t", [P, KC, T])
        h_hi = sb("h_hi", [P, KC, T], F32R)
        h_lo = sb("h_lo", [P, KC, T], F32R)
        bn = sb("bn", [P, 2, TILES, 6])
        mv = sb("mv", [P, 2, TILES, 2])
        ve = sb("ve", [P, 2, TILES])
        rstd = sb("rstd", [P, 2, TILES])
        minus_half = sb("minus_half", [P, TILES])
        amax_x = sb("amax_x", [P, TILES, KC])
        safe_x = sb("safe_x", [P, TILES, KC])
        inv_x = sb("inv_x", [P, TILES, KC])
        mul_x = sb("mul_x", [P, TILES, KC])
        deq_x = sb("deq_x", [P, TILES, KC])
        amax_c = sb("amax_c", [P, HALVES, HB * KC * 2])
        CB = HB * KC * 2
        blk_c = sb("blk_c", [CB, HALVES, 4])
        diag = sb("diag", [CB, HALVES, 2 * CB])
        scl_c = sb("scl_c", [P, HALVES, 2 * CB])
        deq = sb("deq", [P, TILES, KC, 2])
        g_raw = sb("g_raw", [P, 2])
        g_tanh = sb("g_tanh", [P, 2])
        gate_raw = sb("gate_raw", [P, KC, GP])
        gate_hi = sb("gate_hi", [P, KC, GP], F32R)
        gate_lo = sb("gate_lo", [P, KC, GP], F32R)
        lg = sb("lg", [P, HT, GP])
        lmax = sb("lmax", [P, HT])
        ex_in = sb("ex_in", [P, HT, G])
        ex = sb("ex", [P, HT, G])
        gt = sb("gt", [P, HT, E, E])
        eq = sb("eq", [P, HT, E, E])
        before = sb("before", [P, E, E])
        rank = sb("rank", [P, HT, E])
        wsum = sb("wsum", [P, HT, 2])
        comb = sb("comb", [P, HT, G])
        rest = sb("rest", [P, HT, G])
        comb_parts = sb("comb_parts", [P, HT, P], BF16)
        comb_t = sb("comb_t", [P, HALVES, HN], BF16)
        spread = sb("spread", [P, UNITS * P], F16)
        w_raw = sb("w_raw", [P, UNITS, WC])
        w_hi = sb("w_hi", [P, 2, WC], F32R)
        w_lo = sb("w_lo", [P, 2, WC], F32R)
        silu = sb("silu", [P, 2, HN])
        act = sb("act", [P, HN])
        a_hi = sb("a_hi", [P, 2, HN], F32R)
        a_lo = sb("a_lo", [P, 2, HN], F32R)
        fin = sb("fin", [P, 2, HN])
        eye = sb("eye", [P, P])
        eye_b = sb("eye_b", [P, P], BF16)
        ones = sb("ones", [CB, P])

        bank = [stack.enter_context(nc.psum_tensor(f"bank{i}", [P, HN], F32)) for i in range(8)]
        BLK, QT, LOGIT, COMBT = bank[0], bank[7], bank[5], bank[6]
        ATT, Y2T, X1T = bank[1:5], bank[1:3], bank[3:5]
        GATE, UP, MIX, OUT = bank[0:2], bank[2:4], bank[4:6], bank[6:8]
        qt_b = QT[:].bitcast(BF16).rearrange("p (k t) -> p k t", k=KC)
        combt_b = COMBT[:].bitcast(BF16)[:, 0:HN]

        x_landed = [sem(f"x_landed{h}") for h in range(HALVES)]
        ctx_landed = [sem(f"ctx_landed{h}") for h in range(HALVES)]
        gates_landed = sem("gates_landed")
        gate_w_landed = sem("gate_w_landed")
        sel_landed = sem("sel_landed")
        w_landed = [sem(f"w_landed{i}") for i in range(2)]
        stored = sem("stored")
        consts, ident_filled, spread_zeroed = sem("consts"), sem("ident_filled"), sem("spread_zeroed")
        tanh_done, gate_hi_done, gate_split = sem("tanh_done"), sem("gate_hi_done"), sem("gate_split")
        dve_did = sem("dve_did")
        ctx_amax, ctx_amax_t, ctx_diag = sem("ctx_amax"), sem("ctx_amax_t"), sem("ctx_diag")
        ctx_scales, ctx_scaled_ready, vc_ready = sem("ctx_scales"), sem("ctx_scaled_ready"), sem("vc_ready")
        var_ready, rstd_ready = sem("var_ready"), sem("rstd_ready")
        mul_x_ready, vx_ready = sem("mul_x_ready"), sem("vx_ready")
        xq_ready, xqt_psum, xqt_ready = sem("xq_ready"), sem("xqt_psum"), sem("xqt_ready")
        cq_ready, att_ready, x1_ready = sem("cq_ready"), sem("att_ready"), sem("x1_ready")
        var1_ready, rstd1_ready, y2_ready = sem("var1_ready"), sem("rstd1_ready"), sem("y2_ready")
        x1t_psum, x1t_copied = sem("x1t_psum"), sem("x1t_copied")
        y2t_psum, h_hi_done, h_lo_done = sem("y2t_psum"), sem("h_hi_done"), sem("h_lo_done")
        logits_ready, ex_in_ready, ex_ready = sem("logits_ready"), sem("ex_in_ready"), sem("ex_ready")
        comb_split, comb_psum, comb_ready = sem("comb_split"), sem("comb_psum"), sem("comb_ready")
        gu_hi_done, gu_lo_done = sem("gu_hi_done"), sem("gu_lo_done")
        d_hi_done, d_lo_done = sem("d_hi_done"), sem("d_lo_done")
        gate_done, up_done, silu_done = sem("gate_done"), sem("up_done"), sem("silu_done")
        gated_done, act_done, a_hi_done = sem("gated_done"), sem("act_done"), sem("a_hi_done")
        half_done, fin_done = sem("half_done"), sem("fin_done")

        def tiles(h):
            return range(HT * h, HT * (h + 1))

        block = stack.enter_context(nc.Block())

        @block.sync
        def _(sp):
            for h in range(HALVES):
                sp.dma_start(x[:, HT * h:HT * (h + 1), :], xs[:, HT * h:HT * (h + 1), :]).then_inc(x_landed[h], 16)
            for c in range(UNITS):
                if c >= 2:
                    sp.wait_ge(w_landed[c % 2], 16 * (c // 2))
                if c < FULL:
                    sp.dma_start(w_raw[:, c, :], w_full[c]).then_inc(w_landed[c % 2], 16)
                else:
                    sp.dma_start(w_raw[:, c, 0:GUL + D], w_last).then_inc(w_landed[c % 2], 16)
            for n in range(HALVES * KC):
                h, k = n // KC, n % KC
                sp.wait_ge(fin_done, n + 1)
                sp.dma_start(out_t[k, :, h * HN:(h + 1) * HN], fin[:, k, :]).then_inc(stored, 16)
            sp.wait_ge(stored, 16 * HALVES * KC)

        @block.gpsimd
        def _(pool):
            nc.gpsimd.memset(eye[:], 0.0).then_inc(ident_filled, 1)
            nc.gpsimd.memset(minus_half[:], -0.5)
            nc.gpsimd.memset(ones[:], 1.0)
            pool.wait_ge(ident_filled, 1)
            nc.gpsimd.affine_select(out=eye[:], in_=eye[:], compare_op=ALU.not_equal, fill=1.0, base=0,
                                    pattern=[[-1, P]], channel_multiplier=1).then_inc(ident_filled, 1)
            nc.gpsimd.memset(before[:], 0.0).then_inc(ident_filled, 1)
            pool.wait_ge(ident_filled, 3)
            nc.gpsimd.affine_select(out=before[:], in_=before[:], compare_op=ALU.is_ge, fill=1.0, base=0,
                                    pattern=[[-1, E], [1, E]], channel_multiplier=0)
            nc.gpsimd.tensor_copy(eye_b[:], eye[:])
            nc.gpsimd.memzero(comb_parts[:]).then_inc(consts, 1)
            nc.gpsimd.memzero(spread[:]).then_inc(spread_zeroed, 1)
            for h in range(HALVES):
                pool.wait_ge(var_ready, h + 1)
                nc.gpsimd.tensor_tensor(rstd[:, 0, HT * h:HT * (h + 1)], ve[:, 0, HT * h:HT * (h + 1)],
                                        minus_half[:, 0:HT], ALU.pow).then_inc(rstd_ready, 1)
                pool.wait_ge(ctx_scaled_ready, h + 1)
                for i in range(CB):
                    b, k, n = HB * h + i // (2 * KC), i // 2 % KC, i % 2
                    last = nc.gpsimd.tensor_scalar(cw[:, b, k, n, :], cw[:, b, k, n, :], scl_c[:, h, i:i + 1],
                                                   None, ALU.mult)
                last.then_inc(vc_ready, 1)
            for h in range(HALVES):
                pool.wait_ge(var1_ready, h + 1)
                nc.gpsimd.tensor_tensor(rstd[:, 1, HT * h:HT * (h + 1)], ve[:, 1, HT * h:HT * (h + 1)],
                                        minus_half[:, 0:HT], ALU.pow).then_inc(rstd1_ready, 1)

        @block.scalar
        def _(a):
            for h in range(HALVES):
                a.dma_start(cw[:, HB * h:HB * (h + 1)], ctx_t[:, HB * h:HB * (h + 1)]).then_inc(ctx_landed[h], 16)
            a.dma_start(g_raw[:, 0:1], g_x.to_broadcast((P, 1))).then_inc(gates_landed, 16)
            a.dma_start(g_raw[:, 1:2], g_f.to_broadcast((P, 1))).then_inc(gates_landed, 16)
            a.dma_start(gate_raw[:], gate_t).then_inc(gate_w_landed, 16)
            a.wait_ge(spread_zeroed, 1)
            a.dma_start(spread[0:3 * G, 0:ROWS], sel).then_inc(sel_landed, 16)
            a.wait_ge(gates_landed, 32)
            nc.scalar.activation(g_tanh[:], g_raw[:], ACT.Tanh).then_inc(tanh_done, 1)
            a.wait_ge(gate_w_landed, 16)
            nc.scalar.activation(gate_hi[:], gate_raw[:], ACT.Copy).then_inc(gate_hi_done, 1)

            def scale_x(h):
                a.wait_ge(mul_x_ready, h + 1)
                for j in tiles(h):
                    for k in range(KC):
                        last = nc.scalar.activation(xc[:, j, k, :], xc[:, j, k, :], ACT.Copy,
                                                    scale=mul_x[:, j, k:k + 1])
                last.then_inc(vx_ready, 1)

            def copy_xqt(h):
                a.wait_ge(xqt_psum, h + 1)
                nc.scalar.activation(xqt[:, h], qt_b, ACT.Copy).then_inc(xqt_ready, 1)

            def copy_x1t(h):
                for k in range(KC):
                    a.wait_ge(x1t_psum, KC * h + k + 1)
                    nc.scalar.activation(x1t[:, k, h * HN:(h + 1) * HN], X1T[k][:], ACT.Copy).then_inc(x1t_copied, 1)

            def high_h(h):
                for k in range(KC):
                    a.wait_ge(y2t_psum, KC * h + k + 1)
                    nc.scalar.activation(h_hi[:, k, h * HN:(h + 1) * HN], Y2T[k][:], ACT.Copy).then_inc(h_hi_done, 1)

            def exp_router(h):
                a.wait_ge(ex_in_ready, h + 1)
                nc.scalar.activation(ex[:], ex_in[:], ACT.Exp).then_inc(ex_ready, 1)

            def copy_comb(h):
                a.wait_ge(comb_psum, h + 1)
                nc.scalar.activation(comb_t[:, h], combt_b, ACT.Copy).then_inc(comb_ready, 1)

            scale_x(0)
            scale_x(1)
            copy_xqt(0)
            copy_xqt(1)
            for h in range(HALVES):
                copy_x1t(h)
                high_h(h)
                exp_router(h)
                copy_comb(h)

            def high_gu(c, slot, cols=GU):
                nc.scalar.activation(w_hi[:, slot, 0:cols], w_raw[:, bass.ds(c, 1), 0:cols], ACT.Copy)\
                    .then_inc(gu_hi_done, 1)

            def high_d(c, slot, rows=P, at=GU):
                nc.scalar.activation(w_hi[0:rows, slot, GU:WC], w_raw[0:rows, bass.ds(c, 1), at:at + D], ACT.Copy)\
                    .then_inc(d_hi_done, 1)

            def silu_unit(n, slot, rows=P):
                a.wait_ge(gate_done, n + 1)
                nc.scalar.activation(silu[0:rows, slot, :], GATE[slot][0:rows, :], ACT.Silu).then_inc(silu_done, 1)

            a.wait_ge(w_landed[0], 16)
            high_gu(0, 0)
            for h in range(HALVES):
                n0 = UNITS * h

                def unit(c, s, landed=None):
                    slot = (s + h) % 2
                    silu_unit(n0 + c, slot)
                    if h == 0:
                        a.wait_ge(w_landed[(s + 1) % 2], landed)
                    high_gu(c + 1, 1 - slot)
                    high_d(c, slot)

                with a.Fori(0, FULL // 2 - 1) as j:
                    unit(2 * j, 0, 16 * j + 16)
                    unit(2 * j + 1, 1, 16 * j + 32)
                unit(FULL - 2, 0, 16 * (FULL // 2))
                slot = (1 + h) % 2
                silu_unit(n0 + FULL - 1, slot)
                if h == 0:
                    a.wait_ge(w_landed[0], 16 * (FULL // 2 + 1))
                high_gu(FULL, 1 - slot, GUL)
                high_d(FULL - 1, slot)
                silu_unit(n0 + FULL, 1 - slot, LAST)
                if h + 1 < HALVES:
                    high_gu(0, slot)
                high_d(FULL, 1 - slot, LAST, GUL)

        @block.vector
        def _(v):
            steps = [0]

            def did(ins):
                steps[0] += 1
                ins.then_inc(dve_did, 1)
                return steps[0]

            def after(step):
                v.wait_ge(dve_did, step)

            def max_ctx(h):
                v.wait_ge(ctx_landed[h], 16)
                nc.vector.tensor_reduce(amax_c[:, h, :], cw[:, HB * h:HB * (h + 1)].rearrange("p b k n c -> p (b k n) c"),
                                        op=ALU.max, axis=AX.X, apply_absolute_value=True).then_inc(ctx_amax, 1)

            def stats(which, src, h):
                for j in tiles(h):
                    last = nc.vector.bn_stats(bn[:, which, j, :], src[:, j, :])
                after(did(last))
                for j in tiles(h):
                    last = nc.vector.bn_aggr(mv[:, which, j, :], bn[:, which, j, :])
                after(did(last))
                return nc.vector.tensor_scalar(ve[:, which, HT * h:HT * (h + 1)], mv[:, which, HT * h:HT * (h + 1), 1],
                                               LN_EPS, None, ALU.add)

            def centre_x(h):
                v.wait_ge(x_landed[h], 16)
                stats(0, x, h).then_inc(var_ready, 1)
                for j in tiles(h):
                    last = nc.vector.tensor_scalar(xc[:, j].rearrange("p k c -> p (k c)"), x[:, j, :], mv[:, 0, j, 0:1],
                                                   None, ALU.subtract)
                after(did(last))
                return did(nc.vector.tensor_reduce(amax_x[:, HT * h:HT * (h + 1), :], xc[:, HT * h:HT * (h + 1)],
                                                   op=ALU.max, axis=AX.X, apply_absolute_value=True))

            def block_scales_ctx(h):
                v.wait_ge(ctx_amax_t, h + 1)
                after(did(nc.vector.tensor_reduce(blk_c[:, h, 0:1], BLK[0:CB, 0:P], op=ALU.max, axis=AX.X)))
                after(did(nc.vector.tensor_scalar(blk_c[:, h, 1:2], blk_c[:, h, 0:1], W_EPS, None, ALU.max)))
                after(did(nc.vector.reciprocal(blk_c[:, h, 2:3], blk_c[:, h, 1:2])))
                nc.vector.tensor_scalar(diag[:, h, 0:CB], eye[0:CB, 0:CB], blk_c[:, h, 2:3], FP8_MAX, ALU.mult, ALU.mult)
                nc.vector.tensor_scalar(diag[:, h, CB:2 * CB], eye[0:CB, 0:CB], blk_c[:, h, 1:2], 1.0 / FP8_MAX,
                                        ALU.mult, ALU.mult).then_inc(ctx_diag, 1)

            def copy_scales_ctx(h):
                v.wait_ge(ctx_scales, h + 1)
                nc.vector.tensor_copy(scl_c[:, h, :], BLK[:, P:P + 2 * CB]).then_inc(ctx_scaled_ready, 1)

            def scales_x(h, amax_step):
                hs = slice(HT * h, HT * (h + 1))
                r = rstd[:, 0, hs].unsqueeze(2).to_broadcast((P, HT, KC))
                v.wait_ge(rstd_ready, h + 1)
                after(amax_step)
                after(did(nc.vector.tensor_tensor(safe_x[:, hs], amax_x[:, hs], r, ALU.mult)))
                after(did(nc.vector.tensor_scalar(safe_x[:, hs], safe_x[:, hs], ACT_EPS, None, ALU.max)))
                after(did(nc.vector.reciprocal(inv_x[:, hs], safe_x[:, hs])))
                after(did(nc.vector.tensor_scalar(inv_x[:, hs], inv_x[:, hs], FP8_MAX, None, ALU.mult)))
                nc.vector.tensor_tensor(mul_x[:, hs], inv_x[:, hs], r, ALU.mult).then_inc(mul_x_ready, 1)
                v.wait_ge(tanh_done, 1)
                return did(nc.vector.tensor_scalar(deq_x[:, hs], safe_x[:, hs], 1.0 / FP8_MAX, g_tanh[:, 0:1],
                                                   ALU.mult, ALU.mult))

            def round_fp8(val, mag, quantised):
                after(did(nc.vector.tensor_scalar(mag.bitcast(I32), val.bitcast(I32), EXP_BITS, None, ALU.bitwise_and)))
                after(did(nc.vector.tensor_scalar(mag, mag, SUBNORMAL, MAGIC, ALU.max, ALU.mult)))
                after(did(nc.vector.tensor_tensor(val, val, mag, ALU.add)))
                return nc.vector.tensor_tensor(quantised, val, mag, ALU.subtract)

            def quantise_ctx(h):
                hs = slice(HB * h, HB * (h + 1))
                v.wait_ge(vc_ready, h + 1)
                flat = "p b k n c -> p (b k n c)"
                round_fp8(cw[:, hs].rearrange(flat), ce[:, hs].rearrange(flat),
                          cq[:, hs].rearrange("p b k c -> p (b k c)")).then_inc(cq_ready, 1)

            def quantise_x(h):
                hs = slice(HT * h, HT * (h + 1))
                v.wait_ge(vx_ready, h + 1)
                flat = "p j k c -> p (j k c)"
                round_fp8(xc[:, hs].rearrange(flat), xe[:, hs].rearrange(flat),
                          xq[:, hs].rearrange(flat)).then_inc(xq_ready, 1)

            def dequant_scales(h, deq_step):
                after(deq_step)
                back = scl_c[:, h, CB:2 * CB].rearrange("p (b k n) -> p b k n", b=HB, k=KC)
                for i in range(HB):
                    js = slice(HT * h + 2 * i, HT * h + 2 * i + 2)
                    for k in range(KC):
                        last = nc.vector.tensor_tensor(deq[:, js, k, :], deq_x[:, js, k].unsqueeze(2).to_broadcast((P, 2, 2)),
                                                       back[:, i, k, :].unsqueeze(1).to_broadcast((P, 2, 2)), ALU.mult)
                return did(last)

            def residual(h, deq_step):
                after(deq_step)
                first = []
                for jj, j in enumerate(tiles(h)):
                    v.wait_ge(att_ready, j + 1)
                    for n in range(2):
                        ns = slice(n * P, (n + 1) * P)
                        last = nc.vector.scalar_tensor_tensor(x1[:, j, ns], ATT[jj][:, ns], deq[:, j, 0, n:n + 1], x[:, j, ns],
                                                              ALU.mult, ALU.add)
                    first.append(did(last))
                for jj, j in enumerate(tiles(h)):
                    after(first[jj])
                    for n in range(2):
                        ns = slice(n * P, (n + 1) * P)
                        last = nc.vector.scalar_tensor_tensor(x1[:, j, ns], ATT[jj][:, D + n * P:D + (n + 1) * P],
                                                              deq[:, j, 1, n:n + 1], x1[:, j, ns], ALU.mult, ALU.add)
                    last.then_inc(x1_ready, 1)

            def stats_x1(h):
                v.wait_ge(x1_ready, HT * (h + 1))
                stats(1, x1, h).then_inc(var1_ready, 1)

            def norm_x1(h):
                v.wait_ge(rstd1_ready, h + 1)
                for j in tiles(h):
                    nc.vector.tensor_scalar(y2[:, j, :], x1[:, j, :], mv[:, 1, j, 0:1], rstd[:, 1, j:j + 1],
                                            ALU.subtract, ALU.mult).then_inc(y2_ready, 1)

            def low_h(h):
                for k in range(KC):
                    ts = slice(h * HN, (h + 1) * HN)
                    v.wait_ge(h_hi_done, KC * h + k + 1)
                    nc.vector.tensor_tensor(h_lo[:, k, ts], Y2T[k][:], h_hi[:, k, ts].bitcast(F32), ALU.subtract)\
                        .then_inc(h_lo_done, 1)

            def split_gate_w():
                v.wait_ge(gate_hi_done, 1)
                nc.vector.tensor_tensor(gate_lo[:], gate_raw[:], gate_hi[:].bitcast(F32), ALU.subtract)\
                    .then_inc(gate_split, 1)

            def route(h):
                v.wait_ge(logits_ready, h + 1)
                after(did(nc.vector.tensor_copy(lg[:], LOGIT[:, 0:HT * GP].rearrange("p (j g) -> p j g", j=HT))))
                l = lg[:, :, 0:E]
                li = l.unsqueeze(3).to_broadcast((P, HT, E, E))
                lj = l.unsqueeze(2).to_broadcast((P, HT, E, E))
                after(did(nc.vector.tensor_reduce(lmax[:], l, op=ALU.max, axis=AX.X)))
                nc.vector.tensor_tensor(ex_in[:, :, 0:E], l, lmax[:].unsqueeze(2).to_broadcast((P, HT, E)), ALU.subtract)
                nc.vector.tensor_scalar(ex_in[:, :, E:G], lg[:, :, E:G], -1.0, None, ALU.mult).then_inc(ex_in_ready, 1)
                nc.vector.tensor_tensor(gt[:], lj, li, ALU.is_gt)
                after(did(nc.vector.tensor_tensor(eq[:], lj, li, ALU.is_equal)))
                after(did(nc.vector.tensor_tensor(eq[:], eq[:], before[:].unsqueeze(1).to_broadcast((P, HT, E, E)), ALU.mult)))
                after(did(nc.vector.tensor_tensor(gt[:], gt[:], eq[:], ALU.add)))
                after(did(nc.vector.tensor_reduce(rank[:], gt[:], op=ALU.add, axis=AX.X)))
                v.wait_ge(ex_ready, h + 1)
                chosen = did(nc.vector.scalar_tensor_tensor(comb[:, :, 0:E], rank[:], TOP - 0.5, ex[:, :, 0:E], ALU.is_lt, ALU.mult))
                nc.vector.tensor_scalar(wsum[:, :, 1], ex[:, :, E], 1.0, None, ALU.add)
                after(chosen)
                after(did(nc.vector.tensor_reduce(wsum[:, :, 0:1], comb[:, :, 0:E], op=ALU.add, axis=AX.X)))
                after(did(nc.vector.reciprocal(wsum[:], wsum[:])))
                nc.vector.tensor_tensor(comb[:, :, 0:E], comb[:, :, 0:E], wsum[:, :, 0:1].to_broadcast((P, HT, E)), ALU.mult)
                after(did(nc.vector.tensor_copy(comb[:, :, E:G], wsum[:, :, 1:2])))
                if h >= 1:
                    v.wait_ge(comb_psum, h)
                after(did(nc.vector.tensor_copy(comb_parts[:, :, 0:G], comb[:])))
                after(did(nc.vector.tensor_tensor(rest[:], comb[:], comb_parts[:, :, 0:G], ALU.subtract)))
                after(did(nc.vector.tensor_copy(comb_parts[:, :, G:2 * G], rest[:])))
                nc.vector.tensor_tensor(comb_parts[:, :, 2 * G:3 * G], rest[:], comb_parts[:, :, G:2 * G], ALU.subtract)\
                    .then_inc(comb_split, 1)

            max_ctx(0)
            ax0 = centre_x(0)
            v.wait_ge(consts, 1)
            block_scales_ctx(0)
            dx0 = scales_x(0, ax0)
            copy_scales_ctx(0)
            max_ctx(1)
            ax1 = centre_x(1)
            quantise_x(0)
            block_scales_ctx(1)
            dx1 = scales_x(1, ax1)
            quantise_ctx(0)
            copy_scales_ctx(1)
            dq0 = dequant_scales(0, dx0)
            split_gate_w()
            residual(0, dq0)
            stats_x1(0)
            quantise_x(1)
            norm_x1(0)
            quantise_ctx(1)
            low_h(0)
            dq1 = dequant_scales(1, dx1)
            route(0)
            residual(1, dq1)
            stats_x1(1)
            norm_x1(1)
            low_h(1)
            route(1)

            def low_gu(n, c, slot, cols=GU):
                v.wait_ge(gu_hi_done, n + 1)
                nc.vector.tensor_tensor(w_lo[:, slot, 0:cols], w_raw[:, bass.ds(c, 1), 0:cols],
                                        w_hi[:, slot, 0:cols].bitcast(F32), ALU.subtract).then_inc(gu_lo_done, 1)

            def low_d(n, c, slot, rows=P, at=GU):
                v.wait_ge(d_hi_done, n + 1)
                nc.vector.tensor_tensor(w_lo[0:rows, slot, GU:WC], w_raw[0:rows, bass.ds(c, 1), at:at + D],
                                        w_hi[0:rows, slot, GU:WC].bitcast(F32), ALU.subtract).then_inc(d_lo_done, 1)

            def gated(n, slot, rows=P, up=None):
                up = UP[slot][:] if up is None else up
                v.wait_ge(silu_done, n + 1)
                v.wait_ge(up_done, n + 1)
                nc.vector.tensor_tensor(silu[0:rows, slot, :], silu[0:rows, slot, :], up, ALU.mult).then_inc(gated_done, 1)
                v.wait_ge(gated_done, n + 1)
                nc.vector.tensor_tensor(act[0:rows, :], silu[0:rows, slot, :], MIX[slot][0:rows, :], ALU.mult)\
                    .then_inc(act_done, 1)
                v.wait_ge(act_done, n + 1)
                nc.vector.tensor_copy(a_hi[0:rows, slot, :], act[0:rows, :]).then_inc(a_hi_done, 1)
                v.wait_ge(a_hi_done, n + 1)
                nc.vector.tensor_tensor(a_lo[0:rows, slot, :], act[0:rows, :], a_hi[0:rows, slot, :].bitcast(F32),
                                        ALU.subtract)

            def finish(h):
                for k in range(KC):
                    v.wait_ge(half_done, KC * h + k + 1)
                    if h >= 1:
                        v.wait_ge(stored, 16 * KC * h)
                    nc.vector.scalar_tensor_tensor(fin[:, k, :], OUT[k][:], g_tanh[:, 1:2], x1t[:, k, h * HN:(h + 1) * HN],
                                                   ALU.mult, ALU.add).then_inc(fin_done, 1)

            low_gu(0, 0, 0)
            for h in range(HALVES):
                n0 = UNITS * h

                def unit(c, s):
                    slot = (s + h) % 2
                    low_gu(n0 + c + 1, c + 1, 1 - slot)
                    gated(n0 + c, slot)
                    low_d(n0 + c, c, slot)

                if h >= 1:
                    unit(0, 0)
                    finish(h - 1)
                    unit(1, 1)
                with v.Fori(1 if h else 0, FULL // 2 - 1) as j:
                    unit(2 * j, 0)
                    unit(2 * j + 1, 1)
                unit(FULL - 2, 0)
                slot = (1 + h) % 2
                n = n0 + FULL
                low_gu(n, FULL, 1 - slot, GUL)
                gated(n - 1, slot)
                low_d(n - 1, FULL - 1, slot)
                if h + 1 < HALVES:
                    low_gu(n + 1, 0, slot)
                gated(n, 1 - slot, LAST, GATE[1 - slot][LAST:2 * LAST, :])
                low_d(n, FULL, 1 - slot, LAST, GUL)
            finish(HALVES - 1)

        @block.tensor
        def _(pe):
            def ctx_block_max(h):
                pe.wait_ge(ctx_amax, h + 1)
                if h == 0:
                    pe.wait_ge(consts, 1)
                else:
                    pe.wait_ge(ctx_scaled_ready, h)
                nc.tensor.transpose(BLK[0:CB, 0:P], amax_c[:, h, :], eye[:]).then_inc(ctx_amax_t, 1)

            def ctx_scale_rows(h):
                pe.wait_ge(ctx_diag, h + 1)
                nc.tensor.matmul(BLK[:, P:P + 2 * CB], ones[:], diag[:, h, :], start=True, stop=True).then_inc(ctx_scales, 1)

            def transpose_xq(h):
                pe.wait_ge(xq_ready, h + 1)
                if h >= 1:
                    pe.wait_ge(xqt_ready, h)
                for jj, j in enumerate(tiles(h)):
                    for k in range(KC):
                        last = nc.tensor.transpose(qt_b[:, k, jj * P:(jj + 1) * P], xq[:, j, k, :], eye_b[:])
                last.then_inc(xqt_psum, 1)

            def attend(h):
                pe.wait_ge(xqt_ready, h + 1)
                pe.wait_ge(cq_ready, h + 1)
                if h >= 1:
                    pe.wait_ge(h_lo_done, KC * h)
                    pe.wait_ge(x1t_copied, KC * h)
                for jj, j in enumerate(tiles(h)):
                    for k in range(KC):
                        last = nc.tensor.matmul(ATT[jj][:, k * D:(k + 1) * D], xqt[:, h, k, jj * P:(jj + 1) * P],
                                                cq[:, j // 2, k, :], start=True, stop=True)
                    last.then_inc(att_ready, 1)

            def transpose_tokens(h, src, dst, done):
                for k in range(KC):
                    for jj, j in enumerate(tiles(h)):
                        last = nc.tensor.transpose(dst[k][:, jj * P:(jj + 1) * P], src[:, j, k * P:(k + 1) * P], eye[:])
                    last.then_inc(done, 1)

            def router(h):
                pe.wait_ge(gate_split, 1)
                pe.wait_ge(h_lo_done, KC * (h + 1))
                if h >= 1:
                    pe.wait_ge(ex_in_ready, h)
                for jj, j in enumerate(tiles(h)):
                    ts = slice(j * P, (j + 1) * P)
                    for k in range(KC):
                        for i, (lhs, rhs) in enumerate(((h_hi, gate_hi), (h_hi, gate_lo), (h_lo, gate_hi))):
                            last = nc.tensor.matmul(LOGIT[:, jj * GP:(jj + 1) * GP], lhs[:, k, ts], rhs[:, k, :],
                                                    start=(k == 0 and i == 0), stop=(k == KC - 1 and i == 2))
                last.then_inc(logits_ready, 1)

            def transpose_comb(h):
                pe.wait_ge(comb_split, h + 1)
                if h >= 1:
                    pe.wait_ge(comb_ready, h)
                for jj in range(HT):
                    last = nc.tensor.transpose(combt_b[:, jj * P:(jj + 1) * P], comb_parts[:, jj, :], eye_b[:])
                last.then_inc(comb_psum, 1)

            ctx_block_max(0)
            ctx_scale_rows(0)
            ctx_block_max(1)
            transpose_xq(0)
            ctx_scale_rows(1)
            attend(0)
            for h in range(HALVES):
                pe.wait_ge(x1_ready, HT * (h + 1))
                transpose_tokens(h, x1, X1T, x1t_psum)
                if h == 0:
                    transpose_xq(1)
                pe.wait_ge(y2_ready, HT * (h + 1))
                transpose_tokens(h, y2, Y2T, y2t_psum)
                router(h)
                if h == 0:
                    attend(1)
                transpose_comb(h)

            def three_passes(out, w, x_of, start, stop):
                blocks = len(w)
                for k in range(blocks):
                    for i, (a, b) in enumerate(((0, 0), (0, 1), (1, 0))):
                        last = nc.tensor.matmul(out, w[k][a], x_of[k][b], start=(start and k == 0 and i == 0),
                                                stop=(stop and k == blocks - 1 and i == 2))
                return last

            def gate_up(h, n, c, slot, packed=False):
                ts = slice(h * HN, (h + 1) * HN)
                tokens = [(h_hi[:, k, ts], h_lo[:, k, ts]) for k in range(KC)]

                def w(which):
                    at = which * KC * P
                    return [(w_hi[:, slot, at + k * P:at + (k + 1) * P], w_lo[:, slot, at + k * P:at + (k + 1) * P])
                            for k in range(KC)]

                pe.wait_ge(gu_lo_done, n + 1)
                three_passes(GATE[slot][:], w(0), tokens, True, True).then_inc(gate_done, 1)
                rows = LAST if packed else P
                mix = nc.tensor.matmul(MIX[slot][0:rows, :], spread[:, bass.ds(c * P, rows)], comb_t[:, h, :], start=True, stop=True)
                if packed:
                    mix.then_inc(up_done, 1)
                else:
                    three_passes(UP[slot][:], w(1), tokens, True, True).then_inc(up_done, 1)

            def down(n, slot, start=False, stop=False, rows=P):
                pe.wait_ge(d_lo_done, n + 1)
                for k in range(KC):
                    ks = slice(GU + k * P, GU + (k + 1) * P)
                    last = three_passes(OUT[k][:], [(w_hi[0:rows, slot, ks], w_lo[0:rows, slot, ks])],
                                        [(a_hi[0:rows, slot, :], a_lo[0:rows, slot, :])], start, stop)
                    if stop:
                        last.then_inc(half_done, 1)

            pe.wait_ge(sel_landed, 16)
            pe.wait_ge(comb_ready, HALVES)
            pe.wait_ge(x1t_copied, HALVES * KC)
            gate_up(0, 0, 0, 0)
            for h in range(HALVES):
                n0 = UNITS * h
                even, odd = h % 2, (1 + h) % 2
                gate_up(h, n0 + 1, 1, odd)
                if h >= 1:
                    pe.wait_ge(fin_done, KC * h)
                down(n0, even, start=True)
                with pe.Fori(0, FULL // 2 - 1) as j:
                    gate_up(h, n0 + 2 + 2 * j, 2 * j + 2, even)
                    down(n0 + 1 + 2 * j, odd)
                    gate_up(h, n0 + 3 + 2 * j, 2 * j + 3, odd)
                    down(n0 + 2 + 2 * j, even)
                gate_up(h, n0 + FULL, FULL, even, packed=True)
                down(n0 + FULL - 1, odd)
                if h + 1 < HALVES:
                    gate_up(h + 1, n0 + UNITS, 0, odd)
                down(n0 + FULL, even, stop=True, rows=LAST)


def kernel(**inputs):
    import numpy as np
    import concourse.bacc as bacc
    from concourse.bass_utils import run_bass_kernel_spmd

    a = {k: np.asarray(v) for k, v in inputs.items()}
    xs = np.ascontiguousarray(a["x"].reshape(TILES, P, D).transpose(1, 0, 2))
    ctx_t = np.ascontiguousarray(a["ctx_2048"].reshape(B, D, KC, P).transpose(3, 0, 2, 1))
    gate = np.concatenate([a["L0_ffn_gate_w"], a["L0_ffn_shared_gate_w"], np.zeros((GP - G, D), np.float32)])
    gate_t = np.ascontiguousarray(gate.reshape(GP, KC, P).transpose(2, 1, 0))
    gw = np.concatenate([a["L0_ffn_wg"].reshape(E * EI, D), a["L0_ffn_swg"]])
    uw = np.concatenate([a["L0_ffn_wu"].reshape(E * EI, D), a["L0_ffn_swu"]])
    dw = np.concatenate([a["L0_ffn_wd"].transpose(0, 2, 1).reshape(E * EI, D), a["L0_ffn_swd"].T])

    def cols(w, chunks, rows):
        return w.reshape(chunks, rows, KC, P).transpose(0, 3, 2, 1).reshape(chunks, P, KC * rows)

    cut = FULL * P
    w_full = np.ascontiguousarray(np.concatenate(
        [cols(gw[:cut], FULL, P), cols(uw[:cut], FULL, P), dw[:cut].reshape(FULL, P, D)], axis=2))
    last_d = np.concatenate([dw[cut:], np.zeros((P - LAST, D), np.float32)])
    w_last = np.ascontiguousarray(np.concatenate(
        [cols(np.concatenate([gw[cut:], uw[cut:]]), 1, 2 * LAST)[0], last_d], axis=1))
    owner = np.concatenate([np.repeat(np.arange(E), EI), np.full(SI, E)])
    sel = np.ascontiguousarray(np.tile(np.eye(G, dtype=np.float16)[:, owner], (3, 1)))

    arrays = {"xs": xs, "ctx_t": ctx_t, "g_x": a["g_xattn"], "g_f": a["g_ffn"], "gate_t": gate_t,
              "w_full": w_full, "w_last": w_last, "sel": sel}
    nc = bacc.Bacc("TRN2", target_bir_lowering=False, num_devices=1)
    args = [nc.dram_tensor(n, v.shape, mybir.dt.from_np(v.dtype), kind="ExternalInput").ap() for n, v in arrays.items()]
    out_t = nc.dram_tensor("out_t", (KC, P, T), F32, kind="ExternalOutput").ap()
    flamingo_gated_block(nc, *args, out_t)
    r = run_bass_kernel_spmd(nc, [arrays], core_ids=[0])
    got = r.results[0]["out_t"]
    return np.ascontiguousarray(np.asarray(got).reshape(D, T).T).reshape(B, S, D)
```

```python
from contextlib import ExitStack

import concourse.bass as bass
from concourse import mybir

P = 128
B, S, D = 4, 256, 256
T = B * S
TILES = T // P
HALVES = 2
HT = TILES // HALVES
HN = HT * P
HB = B // HALVES
BT = S // P
KC = D // P
E, TOP = 8, 4
EI, SI = 176, 704
ROWS = E * EI + SI
FULL = ROWS // P
LAST = ROWS - FULL * P
UNITS = FULL + 1
G = E + 1
GP = G + 1
GU = 2 * KC * P
WC = GU + D
GUL = KC * P
LN_EPS = 1e-5
FP8_MAX, ACT_EPS, W_EPS = 448.0, 1e-4, 1e-6
EXP_BITS = 0x7F800000
SUBNORMAL = 2.0 ** -6
MAGIC = 1.5 * 2.0 ** 20

F32, F32R = mybir.dt.float32, mybir.dt.float32r
BF16, F16, I32 = mybir.dt.bfloat16, mybir.dt.float16, mybir.dt.int32
ALU = mybir.AluOpType
ACT = mybir.ActivationFunctionType
AX = mybir.AxisListType


def flamingo_gated_block(nc, xs, ctx_t, g_x, g_f, gate_t, w_full, w_last, sel, out_t):
    with ExitStack() as stack:
        def sb(name, shape, dt=F32):
            return stack.enter_context(nc.sbuf_tensor(name, shape, dt))

        def sem(name):
            return stack.enter_context(nc.semaphore(name))

        x = sb("x", [P, TILES, D])
        xc = sb("xc", [P, TILES, KC, P])
        xe = sb("xe", [P, TILES, KC, P])
        xq = sb("xq", [P, TILES, KC, P], BF16)
        xqt = sb("xqt", [P, B, KC, S], BF16)
        cw = sb("cw", [P, B, KC, 2, P])
        ce = sb("ce", [P, B, KC, 2, P])
        cq = sb("cq", [P, B, KC, 2 * P], BF16)
        x1 = sb("x1", [P, TILES, D])
        y2 = sb("y2", [P, TILES, D])
        x1t = sb("x1t", [P, KC, T])
        h_hi = sb("h_hi", [P, KC, T], F32R)
        h_lo = sb("h_lo", [P, KC, T], F32R)
        bn = sb("bn", [P, 2, TILES, 6])
        mv = sb("mv", [P, 2, TILES, 2])
        ve = sb("ve", [P, 2, TILES])
        rstd = sb("rstd", [P, 2, TILES])
        neg_mean = sb("neg_mean", [P, TILES])
        minus_half = sb("minus_half", [P, TILES])
        amax_x = sb("amax_x", [P, TILES, KC])
        safe_x = sb("safe_x", [P, TILES, KC])
        inv_x = sb("inv_x", [P, TILES, KC])
        mul_x = sb("mul_x", [P, TILES, KC])
        deq_x = sb("deq_x", [P, TILES, KC])
        amax_c = sb("amax_c", [P, HALVES, HB * KC * 2])
        CB = HB * KC * 2
        blk_c = sb("blk_c", [CB, HALVES, 4])
        diag = sb("diag", [CB, HALVES, 2 * CB])
        scl_c = sb("scl_c", [P, HALVES, 2 * CB])
        deq = sb("deq", [P, TILES, KC, 2])
        g_raw = sb("g_raw", [P, 2])
        g_tanh = sb("g_tanh", [P, 2])
        gate_raw = sb("gate_raw", [P, KC, P])
        gate_hi = sb("gate_hi", [P, KC, P], F32R)
        gate_lo = sb("gate_lo", [P, KC, P], F32R)
        lg_rows = sb("lg_rows", [GP, HN])
        lg = sb("lg", [P, HT, GP])
        lmax = sb("lmax", [P, HT])
        ex_in = sb("ex_in", [P, HT, G])
        ex = sb("ex", [P, HT, G])
        gt = sb("gt", [P, HT, E, E])
        eq = sb("eq", [P, HT, E, E])
        before = sb("before", [P, E, E])
        rank = sb("rank", [P, HT, E])
        wsum = sb("wsum", [P, HT, 2])
        comb = sb("comb", [P, HT, G])
        rest = sb("rest", [P, HT, G])
        comb_parts = sb("comb_parts", [P, HT, P], BF16)
        comb_t = sb("comb_t", [P, HALVES, HN], BF16)
        spread = sb("spread", [P, UNITS * P], F16)
        w_raw = sb("w_raw", [P, UNITS, WC])
        w_hi = sb("w_hi", [P, 2, WC], F32R)
        w_lo = sb("w_lo", [P, 2, WC], F32R)
        silu = sb("silu", [P, 2, HN])
        act = sb("act", [P, 2, HN])
        a_hi = sb("a_hi", [P, 2, HN], F32R)
        a_lo = sb("a_lo", [P, 2, HN], F32R)
        fin = sb("fin", [P, 2, HN])
        eye = sb("eye", [P, P])
        eye_b = sb("eye_b", [P, P], BF16)
        ones = sb("ones", [CB, P])

        bank = [stack.enter_context(nc.psum_tensor(f"bank{i}", [P, HN], F32)) for i in range(8)]
        GATE, UP, MIX, OUT = bank[0], bank[1], bank[2], bank[3:5]
        QT = [bank[i] for i in (0, 1, 5, 7)]
        ATT = [[bank[i] for i in ks] for ks in ((2, 3), (4, 5), (6, 5), (7, 5))]
        X1T = [bank[i] for i in (6, 2, 6, 7)]
        Y2T = [bank[i] for i in (7, 3, 5, 6)]
        BLK, LOGIT, LOGIT_T, COMBT = ((bank[i], bank[j]) for i, j in ((7, 5), (6, 7), (4, 5), (7, 6)))

        x_landed = [sem(f"x_landed{b}") for b in range(B)]
        ctx_landed = [sem(f"ctx_landed{h}") for h in range(HALVES)]
        gates_landed = sem("gates_landed")
        gate_w_landed = sem("gate_w_landed")
        sel_landed = sem("sel_landed")
        w_landed = [sem(f"w_landed{i}") for i in range(2)]
        stored = sem("stored")
        consts, ident_filled = sem("consts"), sem("ident_filled")
        gate_zeroed, spread_zeroed = sem("gate_zeroed"), sem("spread_zeroed")
        tanh_done, gate_hi_done, gate_split = sem("tanh_done"), sem("gate_hi_done"), sem("gate_split")
        dve_did, pool_did = sem("dve_did"), sem("pool_did")
        ctx_amax, ctx_amax_t, ctx_diag = sem("ctx_amax"), sem("ctx_amax_t"), sem("ctx_diag")
        ctx_scales, ctx_scales_copied = sem("ctx_scales"), sem("ctx_scales_copied")
        ctx_scaled, ctx_magic = sem("ctx_scaled"), sem("ctx_magic")
        cq_ready = [sem(f"cq_ready{b}") for b in range(B)]
        logits_ready, ex_in_ready, ex_ready = sem("logits_ready"), sem("ex_in_ready"), sem("ex_ready")
        logits_copied, logits_t = sem("logits_copied"), sem("logits_t")
        comb_split, comb_psum, comb_ready = sem("comb_split"), sem("comb_psum"), sem("comb_ready")
        var_ready, rstd_ready, centred = sem("var_ready"), sem("rstd_ready"), sem("centred")
        mul_x_ready, x_scaled = sem("mul_x_ready"), sem("x_scaled")
        xq_ready, xqt_psum, xqt_ready = sem("xq_ready"), sem("xqt_psum"), sem("xqt_ready")
        deq_ready, att_ready, res0_ready, x1_ready = sem("deq_ready"), sem("att_ready"), sem("res0_ready"), sem("x1_ready")
        var1_ready, rstd1_ready, y2_ready = sem("var1_ready"), sem("rstd1_ready"), sem("y2_ready")
        x1t_psum, x1t_copied = sem("x1t_psum"), sem("x1t_copied")
        y2t_psum, h_hi_done, h_lo_done = sem("y2t_psum"), sem("h_hi_done"), sem("h_lo_done")
        gu_hi_done, gu_lo_done = sem("gu_hi_done"), sem("gu_lo_done")
        d_hi_done, d_lo_done = sem("d_hi_done"), sem("d_lo_done")
        gate_done, up_done, mix_done, silu_done = sem("gate_done"), sem("up_done"), sem("mix_done"), sem("silu_done")
        gated_done, act_done, a_hi_done, a_lo_done = sem("gated_done"), sem("act_done"), sem("a_hi_done"), sem("a_lo_done")
        half_done, fin_done = sem("half_done"), sem("fin_done")

        def tiles(b):
            return range(BT * b, BT * (b + 1))

        def tile_slice(b):
            return slice(BT * b, BT * (b + 1))

        def batches(h):
            return slice(HB * h, HB * (h + 1))

        def qt_view(b):
            return QT[b][:].bitcast(BF16)[:, 0:KC * S].rearrange("p (k t) -> p k t", k=KC)

        def combt_view(h):
            return COMBT[h][:].bitcast(BF16)[:, 0:HN]

        block = stack.enter_context(nc.Block())

        @block.sync
        def _(sp):
            def load_x(b):
                sp.dma_start(x[:, tile_slice(b), :], xs[:, tile_slice(b), :]).then_inc(x_landed[b], 16)

            load_x(0)
            load_x(1)
            sp.wait_ge(gate_zeroed, 1)
            sp.dma_start(gate_raw[:, :, 0:GP], gate_t).then_inc(gate_w_landed, 16)
            sp.dma_start(g_raw[:, 0:1], g_x.to_broadcast((P, 1))).then_inc(gates_landed, 16)
            sp.dma_start(g_raw[:, 1:2], g_f.to_broadcast((P, 1))).then_inc(gates_landed, 16)
            load_x(2)
            load_x(3)
            sp.dma_start(cw[:, batches(1)], ctx_t[:, batches(1)]).then_inc(ctx_landed[1], 16)
            sp.wait_ge(spread_zeroed, 1)
            sp.dma_start(spread[0:3 * G, 0:ROWS], sel).then_inc(sel_landed, 16)
            for c in range(UNITS):
                if c >= 2:
                    sp.wait_ge(w_landed[c % 2], 16 * (c // 2))
                if c < FULL:
                    sp.dma_start(w_raw[:, c, :], w_full[c]).then_inc(w_landed[c % 2], 16)
                else:
                    sp.dma_start(w_raw[:, c, 0:GUL + D], w_last).then_inc(w_landed[c % 2], 16)
            for n in range(HALVES * KC):
                h, k = n // KC, n % KC
                sp.wait_ge(fin_done, n + 1)
                sp.dma_start(out_t[k, :, h * HN:(h + 1) * HN], fin[:, k, :]).then_inc(stored, 16)
            sp.wait_ge(stored, 16 * HALVES * KC)

        @block.gpsimd
        def _(pool):
            nc.gpsimd.memzero(gate_raw[:]).then_inc(gate_zeroed, 1)
            nc.gpsimd.memset(eye[:], 0.0).then_inc(ident_filled, 1)
            nc.gpsimd.memset(minus_half[:], -0.5)
            nc.gpsimd.memset(ones[:], 1.0)
            pool.wait_ge(ident_filled, 1)
            nc.gpsimd.affine_select(out=eye[:], in_=eye[:], compare_op=ALU.not_equal, fill=1.0, base=0,
                                    pattern=[[-1, P]], channel_multiplier=1).then_inc(ident_filled, 1)
            nc.gpsimd.memset(before[:], 0.0).then_inc(ident_filled, 1)
            pool.wait_ge(ident_filled, 3)
            nc.gpsimd.affine_select(out=before[:], in_=before[:], compare_op=ALU.is_ge, fill=1.0, base=0,
                                    pattern=[[-1, E], [1, E]], channel_multiplier=0)
            nc.gpsimd.tensor_copy(eye_b[:], eye[:])
            nc.gpsimd.memzero(comb_parts[:]).then_inc(consts, 1)
            nc.gpsimd.memzero(spread[:]).then_inc(spread_zeroed, 1)

            def inverse_std(which, b, var_sem, rstd_sem):
                pool.wait_ge(var_sem, b + 1)
                nc.gpsimd.tensor_tensor(rstd[:, which, tile_slice(b)], ve[:, which, tile_slice(b)],
                                        minus_half[:, 0:BT], ALU.pow).then_inc(rstd_sem, 1)

            def add_magic(b):
                pool.wait_ge(ctx_magic, b)
                val = cw[:, b].rearrange("p k n c -> p (k n c)")
                nc.gpsimd.tensor_tensor(val, val, ce[:, b].rearrange("p k n c -> p (k n c)"), ALU.add).then_inc(pool_did, 1)

            def subtract_magic(b):
                pool.wait_ge(pool_did, b)
                nc.gpsimd.tensor_tensor(cq[:, b].rearrange("p k c -> p (k c)"), cw[:, b].rearrange("p k n c -> p (k n c)"),
                                        ce[:, b].rearrange("p k n c -> p (k n c)"), ALU.subtract).then_inc(cq_ready[b], 1)

            def low_gu(n, c, slot, cols=GU):
                pool.wait_ge(gu_hi_done, n + 1)
                nc.gpsimd.tensor_tensor(w_lo[:, slot, 0:cols], w_raw[:, bass.ds(c, 1), 0:cols],
                                        w_hi[:, slot, 0:cols].bitcast(F32), ALU.subtract).then_inc(gu_lo_done, 1)

            def low_d(n, c, slot, rows=P, at=GU):
                pool.wait_ge(d_hi_done, n + 1)
                nc.gpsimd.tensor_tensor(w_lo[0:rows, slot, GU:WC], w_raw[0:rows, bass.ds(c, 1), at:at + D],
                                        w_hi[0:rows, slot, GU:WC].bitcast(F32), ALU.subtract).then_inc(d_lo_done, 1)

            def unit(h, c, s):
                n, slot = UNITS * h + c, (s + h) % 2
                low_gu(n + 1, c + 1, 1 - slot)
                low_d(n, c, slot)

            def last_units(h):
                unit(h, FULL - 2, 0)
                n, slot = UNITS * h + FULL, h % 2
                low_gu(n, FULL, slot, GUL)
                low_d(n - 1, FULL - 1, 1 - slot)
                if h + 1 < HALVES:
                    low_gu(n + 1, 0, 1 - slot)
                low_d(n, FULL, slot, LAST, GUL)

            inverse_std(0, 0, var_ready, rstd_ready)
            inverse_std(0, 1, var_ready, rstd_ready)
            add_magic(1)
            subtract_magic(1)
            inverse_std(1, 0, var1_ready, rstd1_ready)
            inverse_std(1, 1, var1_ready, rstd1_ready)
            low_gu(0, 0, 0)
            inverse_std(0, 2, var_ready, rstd_ready)
            inverse_std(0, 3, var_ready, rstd_ready)
            for c in range(0, 6):
                unit(0, c, c % 2)
            add_magic(2)
            unit(0, 6, 0)
            subtract_magic(2)
            add_magic(3)
            unit(0, 7, 1)
            subtract_magic(3)
            for c in range(8, 11):
                unit(0, c, c % 2)
            inverse_std(1, 2, var1_ready, rstd1_ready)
            unit(0, 11, 1)
            unit(0, 12, 0)
            inverse_std(1, 3, var1_ready, rstd1_ready)
            unit(0, 13, 1)
            last_units(0)
            with pool.Fori(0, FULL // 2 - 1) as j:
                unit(1, 2 * j, 0)
                unit(1, 2 * j + 1, 1)
            last_units(1)

        @block.scalar
        def _(a):
            a.dma_start(cw[:, batches(0)], ctx_t[:, batches(0)]).then_inc(ctx_landed[0], 16)
            a.preload_act_table(ACT.Exp)

            def centre(b):
                a.wait_ge(var_ready, b + 1)
                for j in tiles(b):
                    last = nc.scalar.activation(xc[:, j].rearrange("p k c -> p (k c)"), x[:, j, :], ACT.Identity,
                                                bias=neg_mean[:, j:j + 1])
                last.then_inc(centred, 1)

            def scale_ctx(b):
                h, per = b // HB, 2 * KC
                a.wait_ge(ctx_scales_copied, h + 1)
                for i in range(per):
                    at = (b % HB) * per + i
                    last = nc.scalar.activation(cw[:, b, i // 2, i % 2, :], cw[:, b, i // 2, i % 2, :], ACT.Copy,
                                                scale=scl_c[:, h, at:at + 1])
                last.then_inc(ctx_scaled, 1)

            def scale_x(b):
                a.wait_ge(mul_x_ready, b + 1)
                for j in tiles(b):
                    for k in range(KC):
                        last = nc.scalar.activation(xc[:, j, k, :], xc[:, j, k, :], ACT.Copy,
                                                    scale=mul_x[:, j, k:k + 1])
                last.then_inc(x_scaled, 1)

            def copy_xqt(b):
                a.wait_ge(xqt_psum, b + 1)
                nc.scalar.activation(xqt[:, b], qt_view(b), ACT.Copy).then_inc(xqt_ready, 1)

            def residual0(b):
                a.wait_ge(att_ready, b + 1)
                a.wait_ge(deq_ready, b + 1)
                for jj, j in enumerate(tiles(b)):
                    for n in range(2):
                        last = nc.scalar.activation(y2[:, j, n * P:(n + 1) * P], ATT[b][0][:, jj * D + n * P:jj * D + (n + 1) * P],
                                                    ACT.Copy, scale=deq[:, j, 0, n:n + 1])
                last.then_inc(res0_ready, 1)

            def copy_x1t(b):
                a.wait_ge(x1t_psum, b + 1)
                nc.scalar.activation(x1t[:, :, b * S:(b + 1) * S], X1T[b][:].rearrange("p (k t) -> p k t", k=KC), ACT.Copy)\
                    .then_inc(x1t_copied, 1)

            def high_h(b):
                a.wait_ge(y2t_psum, b + 1)
                nc.scalar.activation(h_hi[:, :, b * S:(b + 1) * S], Y2T[b][:].rearrange("p (k t) -> p k t", k=KC), ACT.Copy)\
                    .then_inc(h_hi_done, 1)

            def copy_logits(h):
                a.wait_ge(logits_ready, h + 1)
                nc.scalar.activation(lg_rows[:], LOGIT[h][0:GP, :], ACT.Copy).then_inc(logits_copied, 1)

            def exp_router(h):
                a.wait_ge(ex_in_ready, h + 1)
                nc.scalar.activation(ex[:], ex_in[:], ACT.Exp).then_inc(ex_ready, 1)

            def copy_comb(h):
                a.wait_ge(comb_psum, h + 1)
                nc.scalar.activation(comb_t[:, h], combt_view(h), ACT.Copy).then_inc(comb_ready, 1)

            def high_gu(c, slot, ups, cols=GU):
                if ups is not None:
                    a.wait_ge(up_done, ups)
                nc.scalar.activation(w_hi[:, slot, 0:cols], w_raw[:, bass.ds(c, 1), 0:cols], ACT.Copy)\
                    .then_inc(gu_hi_done, 1)

            def high_d(c, slot, rows=P, at=GU):
                nc.scalar.activation(w_hi[0:rows, slot, GU:WC], w_raw[0:rows, bass.ds(c, 1), at:at + D], ACT.Copy)\
                    .then_inc(d_hi_done, 1)

            def silu_unit(n, slot, rows=P, bank=GATE):
                a.wait_ge(gate_done, n + 1)
                nc.scalar.activation(silu[0:rows, slot, :], bank[0:rows, :], ACT.Silu).then_inc(silu_done, 1)

            def high_a(n, slot, rows=P):
                a.wait_ge(act_done, n + 1)
                nc.scalar.activation(a_hi[0:rows, slot, :], act[0:rows, slot, :], ACT.Copy).then_inc(a_hi_done, 1)

            def weights(h, c, s, first=False, cols=GU):
                if h == 0:
                    a.wait_ge(w_landed[s], 16 * (c // 2 + 1))
                high_gu(c, (s + h) % 2, None if first else FULL * h + c - 1, cols)

            def silu_and_down(h, c, s):
                silu_unit(UNITS * h + c, (s + h) % 2)
                high_d(c, (s + h) % 2)

            def unit(h, c, s):
                weights(h, c + 1, 1 - s)
                silu_and_down(h, c, s)
                high_a(UNITS * h + c, (s + h) % 2)

            def last_units(h):
                n, slot = UNITS * h + FULL, h % 2
                weights(h, FULL, 0, cols=GUL)
                silu_and_down(h, FULL - 1, 1)
                high_a(n - 1, 1 - slot)
                if h == 0:
                    exp_router(1)
                    high_gu(0, 1 - slot, FULL)
                silu_unit(n, slot, LAST)
                high_d(FULL, slot, LAST, GUL)
                high_a(n, slot, LAST)
                if h == 0:
                    copy_comb(1)

            centre(0)
            scale_x(0)
            centre(1)
            scale_ctx(0)
            scale_ctx(1)
            scale_x(1)
            a.wait_ge(gates_landed, 32)
            nc.scalar.activation(g_tanh[:], g_raw[:], ACT.Tanh).then_inc(tanh_done, 1)
            a.wait_ge(gate_w_landed, 16)
            nc.scalar.activation(gate_hi[:], gate_raw[:], ACT.Copy).then_inc(gate_hi_done, 1)
            copy_xqt(0)
            copy_xqt(1)
            residual0(0)
            residual0(1)
            weights(0, 0, 0, first=True)
            copy_x1t(0)
            copy_x1t(1)
            high_h(0)
            high_h(1)
            weights(0, 1, 1, first=True)
            centre(2)
            high_d(0, 0)
            copy_logits(0)
            centre(3)
            exp_router(0)
            silu_unit(0, 0)
            weights(0, 2, 0)
            silu_unit(1, 1, bank=OUT[0])
            high_d(1, 1)
            copy_comb(0)
            high_a(0, 0)
            weights(0, 3, 1)
            silu_unit(2, 0)
            high_a(1, 1)
            a.wait_ge(mix_done, 3)
            high_d(2, 0)
            high_a(2, 0)
            weights(0, 4, 0)
            silu_and_down(0, 3, 1)
            scale_x(2)
            high_a(3, 1)
            weights(0, 5, 1)
            scale_ctx(2)
            silu_and_down(0, 4, 0)
            scale_x(3)
            high_a(4, 0)
            weights(0, 6, 0)
            scale_ctx(3)
            silu_and_down(0, 5, 1)
            high_a(5, 1)
            unit(0, 6, 0)
            weights(0, 8, 0)
            copy_xqt(2)
            silu_and_down(0, 7, 1)
            high_a(7, 1)
            weights(0, 9, 1)
            copy_xqt(3)
            silu_and_down(0, 8, 0)
            residual0(2)
            high_a(8, 0)
            unit(0, 9, 1)
            weights(0, 11, 1)
            silu_and_down(0, 10, 0)
            residual0(3)
            high_a(10, 0)
            unit(0, 11, 1)
            weights(0, 13, 1)
            copy_x1t(2)
            high_h(2)
            silu_and_down(0, 12, 0)
            high_a(12, 0)
            weights(0, 14, 0)
            copy_x1t(3)
            silu_and_down(0, 13, 1)
            high_h(3)
            high_a(13, 1)
            weights(0, 15, 1)
            silu_and_down(0, 14, 0)
            copy_logits(1)
            high_a(14, 0)
            last_units(0)
            with a.Fori(0, FULL // 2 - 1) as j:
                unit(1, 2 * j, 0)
                unit(1, 2 * j + 1, 1)
            unit(1, FULL - 2, 0)
            last_units(1)

        @block.vector
        def _(v):
            steps = [0]

            def did(ins):
                steps[0] += 1
                ins.then_inc(dve_did, 1)
                return steps[0]

            def after(step):
                v.wait_ge(dve_did, step)

            def max_ctx(h):
                v.wait_ge(ctx_landed[h], 16)
                nc.vector.tensor_reduce(amax_c[:, h, :], cw[:, batches(h)].rearrange("p b k n c -> p (b k n) c"),
                                        op=ALU.max, axis=AX.X, apply_absolute_value=True).then_inc(ctx_amax, 1)

            def stats(which, src, b):
                for j in tiles(b):
                    last = nc.vector.bn_stats(bn[:, which, j, :], src[:, j, :])
                after(did(last))
                for j in tiles(b):
                    last = nc.vector.bn_aggr(mv[:, which, j, :], bn[:, which, j, :])
                after(did(last))
                if which == 0:
                    nc.vector.tensor_scalar(neg_mean[:, tile_slice(b)], mv[:, 0, tile_slice(b), 0], -1.0, None, ALU.mult)
                return nc.vector.tensor_scalar(ve[:, which, tile_slice(b)], mv[:, which, tile_slice(b), 1],
                                               LN_EPS, None, ALU.add)

            def stats_x(b):
                v.wait_ge(x_landed[b], 16)
                stats(0, x, b).then_inc(var_ready, 1)

            def block_scales_ctx(h):
                v.wait_ge(ctx_amax_t, h + 1)
                after(did(nc.vector.tensor_reduce(blk_c[:, h, 0:1], BLK[h][0:CB, 0:P], op=ALU.max, axis=AX.X)))
                after(did(nc.vector.tensor_scalar(blk_c[:, h, 1:2], blk_c[:, h, 0:1], W_EPS, None, ALU.max)))
                after(did(nc.vector.reciprocal(blk_c[:, h, 2:3], blk_c[:, h, 1:2])))
                nc.vector.tensor_scalar(diag[:, h, 0:CB], eye[0:CB, 0:CB], blk_c[:, h, 2:3], FP8_MAX, ALU.mult, ALU.mult)
                nc.vector.tensor_scalar(diag[:, h, CB:2 * CB], eye[0:CB, 0:CB], blk_c[:, h, 1:2], 1.0 / FP8_MAX,
                                        ALU.mult, ALU.mult).then_inc(ctx_diag, 1)

            def copy_scales_ctx(h):
                v.wait_ge(ctx_scales, h + 1)
                nc.vector.tensor_copy(scl_c[:, h, :], BLK[h][:, P:P + 2 * CB]).then_inc(ctx_scales_copied, 1)

            def exponents(mag, val):
                return nc.vector.tensor_scalar(mag.bitcast(I32), val.bitcast(I32), EXP_BITS, None, ALU.bitwise_and)

            def magic_ctx(b):
                v.wait_ge(ctx_scaled, b + 1)
                mag = ce[:, b].rearrange("p k n c -> p (k n c)")
                after(did(exponents(mag, cw[:, b].rearrange("p k n c -> p (k n c)"))))
                return nc.vector.tensor_scalar(mag, mag, SUBNORMAL, MAGIC, ALU.max, ALU.mult)

            def round_ctx_0():
                val = cw[:, 0].rearrange("p k n c -> p (k n c)")
                mag = ce[:, 0].rearrange("p k n c -> p (k n c)")
                after(did(magic_ctx(0)))
                after(did(nc.vector.tensor_tensor(val, val, mag, ALU.add)))
                nc.vector.tensor_tensor(cq[:, 0].rearrange("p k c -> p (k c)"), val, mag, ALU.subtract)\
                    .then_inc(cq_ready[0], 1)

            def max_x(b):
                v.wait_ge(centred, b + 1)
                return did(nc.vector.tensor_reduce(amax_x[:, tile_slice(b), :], xc[:, tile_slice(b)],
                                                   op=ALU.max, axis=AX.X, apply_absolute_value=True))

            def scales_x(b, amax_step):
                js = tile_slice(b)
                r = rstd[:, 0, js].unsqueeze(2).to_broadcast((P, BT, KC))
                v.wait_ge(rstd_ready, b + 1)
                after(amax_step)
                after(did(nc.vector.tensor_tensor(safe_x[:, js], amax_x[:, js], r, ALU.mult)))
                after(did(nc.vector.tensor_scalar(safe_x[:, js], safe_x[:, js], ACT_EPS, None, ALU.max)))
                after(did(nc.vector.reciprocal(inv_x[:, js], safe_x[:, js])))
                nc.vector.scalar_tensor_tensor(mul_x[:, js], inv_x[:, js], FP8_MAX, r, ALU.mult, ALU.mult)\
                    .then_inc(mul_x_ready, 1)

            def magic_x(b):
                v.wait_ge(x_scaled, b + 1)
                mag = xe[:, tile_slice(b)].rearrange("p j k c -> p (j k c)")
                after(did(exponents(mag, xc[:, tile_slice(b)].rearrange("p j k c -> p (j k c)"))))
                return did(nc.vector.tensor_scalar(mag, mag, SUBNORMAL, MAGIC, ALU.max, ALU.mult))

            def round_x(b, magic_step):
                flat = "p j k c -> p (j k c)"
                val, mag = xc[:, tile_slice(b)].rearrange(flat), xe[:, tile_slice(b)].rearrange(flat)
                after(magic_step)
                after(did(nc.vector.tensor_tensor(val, val, mag, ALU.add)))
                nc.vector.tensor_tensor(xq[:, tile_slice(b)].rearrange(flat), val, mag, ALU.subtract).then_inc(xq_ready, 1)

            def dequant_scales(b):
                js, h = tile_slice(b), b // HB
                back = scl_c[:, h, CB:2 * CB].rearrange("p (b k n) -> p b k n", b=HB, k=KC)
                v.wait_ge(tanh_done, 1)
                after(did(nc.vector.tensor_scalar(deq_x[:, js], safe_x[:, js], 1.0 / FP8_MAX, g_tanh[:, 0:1],
                                                  ALU.mult, ALU.mult)))
                for k in range(KC):
                    last = nc.vector.tensor_tensor(deq[:, js, k, :], deq_x[:, js, k].unsqueeze(2).to_broadcast((P, BT, 2)),
                                                   back[:, b % HB, k, :].unsqueeze(1).to_broadcast((P, BT, 2)), ALU.mult)
                last.then_inc(deq_ready, 1)

            def residual1(b):
                v.wait_ge(att_ready, b + 1)
                v.wait_ge(deq_ready, b + 1)
                for jj, j in enumerate(tiles(b)):
                    for n in range(2):
                        ns = slice(n * P, (n + 1) * P)
                        last = nc.vector.scalar_tensor_tensor(x1[:, j, ns], ATT[b][1][:, jj * D + n * P:jj * D + (n + 1) * P],
                                                              deq[:, j, 1, n:n + 1], x[:, j, ns], ALU.mult, ALU.add)
                return did(last)

            def residual_sum(b, step):
                after(step)
                v.wait_ge(res0_ready, b + 1)
                nc.vector.tensor_tensor(x1[:, tile_slice(b), :], x1[:, tile_slice(b), :], y2[:, tile_slice(b), :], ALU.add)\
                    .then_inc(x1_ready, 1)

            def stats_x1(b):
                v.wait_ge(x1_ready, b + 1)
                stats(1, x1, b).then_inc(var1_ready, 1)

            def norm_x1(b):
                v.wait_ge(rstd1_ready, b + 1)
                for j in tiles(b):
                    last = nc.vector.tensor_scalar(y2[:, j, :], x1[:, j, :], mv[:, 1, j, 0:1], rstd[:, 1, j:j + 1],
                                                   ALU.subtract, ALU.mult)
                last.then_inc(y2_ready, 1)

            def low_h(b):
                ts = slice(b * S, (b + 1) * S)
                v.wait_ge(h_hi_done, b + 1)
                nc.vector.tensor_tensor(h_lo[:, :, ts], Y2T[b][:].rearrange("p (k t) -> p k t", k=KC),
                                        h_hi[:, :, ts].bitcast(F32), ALU.subtract).then_inc(h_lo_done, 1)

            def split_gate_w():
                v.wait_ge(gate_hi_done, 1)
                nc.vector.tensor_tensor(gate_lo[:], gate_raw[:], gate_hi[:].bitcast(F32), ALU.subtract)\
                    .then_inc(gate_split, 1)

            def route_choose(h):
                v.wait_ge(logits_t, h + 1)
                after(did(nc.vector.tensor_copy(lg[:], LOGIT_T[h][:, 0:HT * GP].rearrange("p (j g) -> p j g", j=HT))))
                l = lg[:, :, 0:E]
                li = l.unsqueeze(3).to_broadcast((P, HT, E, E))
                lj = l.unsqueeze(2).to_broadcast((P, HT, E, E))
                maxed = did(nc.vector.tensor_reduce(lmax[:], l, op=ALU.max, axis=AX.X))
                equal = did(nc.vector.tensor_tensor(eq[:], lj, li, ALU.is_equal))
                nc.vector.tensor_tensor(gt[:], lj, li, ALU.is_gt)
                after(maxed)
                nc.vector.tensor_tensor(ex_in[:, :, 0:E], l, lmax[:].unsqueeze(2).to_broadcast((P, HT, E)), ALU.subtract)
                nc.vector.tensor_scalar(ex_in[:, :, E:G], lg[:, :, E:G], -1.0, None, ALU.mult).then_inc(ex_in_ready, 1)
                after(equal)
                after(did(nc.vector.tensor_tensor(eq[:], eq[:], before[:].unsqueeze(1).to_broadcast((P, HT, E, E)), ALU.mult)))
                after(did(nc.vector.tensor_tensor(gt[:], gt[:], eq[:], ALU.add)))
                return did(nc.vector.tensor_reduce(rank[:], gt[:], op=ALU.add, axis=AX.X))

            def route_weigh(h, ranked):
                after(ranked)
                v.wait_ge(ex_ready, h + 1)
                chosen = did(nc.vector.scalar_tensor_tensor(comb[:, :, 0:E], rank[:], TOP - 0.5, ex[:, :, 0:E], ALU.is_lt, ALU.mult))
                nc.vector.tensor_scalar(wsum[:, :, 1], ex[:, :, E], 1.0, None, ALU.add)
                after(chosen)
                after(did(nc.vector.tensor_reduce(wsum[:, :, 0:1], comb[:, :, 0:E], op=ALU.add, axis=AX.X)))
                after(did(nc.vector.reciprocal(wsum[:], wsum[:])))
                nc.vector.tensor_tensor(comb[:, :, 0:E], comb[:, :, 0:E], wsum[:, :, 0:1].to_broadcast((P, HT, E)), ALU.mult)
                after(did(nc.vector.tensor_copy(comb[:, :, E:G], wsum[:, :, 1:2])))
                if h >= 1:
                    v.wait_ge(comb_psum, h)
                after(did(nc.vector.tensor_copy(comb_parts[:, :, 0:G], comb[:])))
                after(did(nc.vector.tensor_tensor(rest[:], comb[:], comb_parts[:, :, 0:G], ALU.subtract)))
                after(did(nc.vector.tensor_copy(comb_parts[:, :, G:2 * G], rest[:])))
                nc.vector.tensor_tensor(comb_parts[:, :, 2 * G:3 * G], rest[:], comb_parts[:, :, G:2 * G], ALU.subtract)\
                    .then_inc(comb_split, 1)

            def gated(n, slot, up, ups, rows=P):
                v.wait_ge(silu_done, n + 1)
                if ups is not None:
                    v.wait_ge(up_done, ups)
                nc.vector.tensor_tensor(silu[0:rows, slot, :], silu[0:rows, slot, :], up, ALU.mult).then_inc(gated_done, 1)

            def mixed(n, slot, rows=P):
                v.wait_ge(gated_done, n + 1)
                v.wait_ge(mix_done, n + 1)
                nc.vector.tensor_tensor(act[0:rows, slot, :], silu[0:rows, slot, :], MIX[0:rows, :], ALU.mult)\
                    .then_inc(act_done, 1)

            def low_a(n, slot, rows=P):
                v.wait_ge(a_hi_done, n + 1)
                nc.vector.tensor_tensor(a_lo[0:rows, slot, :], act[0:rows, slot, :], a_hi[0:rows, slot, :].bitcast(F32),
                                        ALU.subtract).then_inc(a_lo_done, 1)

            def unit(h, c, s):
                n, slot = UNITS * h + c, (s + h) % 2
                gated(n, slot, UP[:], FULL * h + c + 1)
                mixed(n, slot)
                low_a(n, slot)

            def last_unit(h):
                n, slot = UNITS * h + FULL, h % 2
                gated(n, slot, GATE[LAST:2 * LAST, :], None, LAST)
                mixed(n, slot, LAST)
                low_a(n, slot, LAST)

            def finish(h):
                for k in range(KC):
                    v.wait_ge(half_done, KC * h + k + 1)
                    if h >= 1:
                        v.wait_ge(stored, 16 * KC * h)
                    nc.vector.scalar_tensor_tensor(fin[:, k, :], OUT[k][:], g_tanh[:, 1:2], x1t[:, k, h * HN:(h + 1) * HN],
                                                   ALU.mult, ALU.add).then_inc(fin_done, 1)

            stats_x(0)
            max_ctx(0)
            max_x_0 = max_x(0)
            scales_x(0, max_x_0)
            stats_x(1)
            v.wait_ge(consts, 1)
            block_scales_ctx(0)
            copy_scales_ctx(0)
            round_x(0, magic_x(0))
            scales_x(1, max_x(1))
            round_ctx_0()
            magic_ctx(1).then_inc(ctx_magic, 1)
            dequant_scales(0)
            round_x(1, magic_x(1))
            residual_sum(0, residual1(0))
            stats_x1(0)
            dequant_scales(1)
            residual_sum(1, residual1(1))
            stats_x1(1)
            norm_x1(0)
            split_gate_w()
            norm_x1(1)
            low_h(0)
            low_h(1)
            stats_x(2)
            stats_x(3)
            max_ctx(1)
            route_weigh(0, route_choose(0))
            gated(0, 0, UP[:], 1)
            gated(1, 1, OUT[1][:], 2)
            mixed(0, 0)
            low_a(0, 0)
            mixed(1, 1)
            low_a(1, 1)
            block_scales_ctx(1)
            unit(0, 2, 0)
            scales_x(2, max_x(2))
            unit(0, 3, 1)
            copy_scales_ctx(1)
            scales_x(3, max_x(3))
            unit(0, 4, 0)
            magic_ctx(2).then_inc(ctx_magic, 1)
            magic_2 = magic_x(2)
            unit(0, 5, 1)
            round_x(2, magic_2)
            magic_ctx(3).then_inc(ctx_magic, 1)
            unit(0, 6, 0)
            round_x(3, magic_x(3))
            unit(0, 7, 1)
            dequant_scales(2)
            dequant_scales(3)
            unit(0, 8, 0)
            part_2 = residual1(2)
            unit(0, 9, 1)
            residual_sum(2, part_2)
            stats_x1(2)
            unit(0, 10, 0)
            norm_x1(2)
            part_3 = residual1(3)
            unit(0, 11, 1)
            residual_sum(3, part_3)
            stats_x1(3)
            unit(0, 12, 0)
            norm_x1(3)
            low_h(2)
            unit(0, 13, 1)
            low_h(3)
            unit(0, 14, 0)
            ranked = route_choose(1)
            unit(0, 15, 1)
            route_weigh(1, ranked)
            last_unit(0)
            unit(1, 0, 0)
            finish(0)
            unit(1, 1, 1)
            with v.Fori(1, FULL // 2) as j:
                unit(1, 2 * j, 0)
                unit(1, 2 * j + 1, 1)
            last_unit(1)
            finish(1)

        @block.tensor
        def _(pe):
            def ctx_block_max(h):
                pe.wait_ge(ctx_amax, h + 1)
                if h == 0:
                    pe.wait_ge(consts, 1)
                else:
                    pe.wait_ge(ex_in_ready, h)
                nc.tensor.transpose(BLK[h][0:CB, 0:P], amax_c[:, h, :], eye[:]).then_inc(ctx_amax_t, 1)

            def ctx_scale_rows(h):
                pe.wait_ge(ctx_diag, h + 1)
                nc.tensor.matmul(BLK[h][:, P:P + 2 * CB], ones[:], diag[:, h, :], start=True, stop=True).then_inc(ctx_scales, 1)

            def transpose_xq(b):
                pe.wait_ge(xq_ready, b + 1)
                if b == 2:
                    pe.wait_ge(ctx_scales_copied, 2)
                if b == 3:
                    pe.wait_ge(comb_ready, 1)
                view = qt_view(b)
                for jj, j in enumerate(tiles(b)):
                    for k in range(KC):
                        last = nc.tensor.transpose(view[:, k, jj * P:(jj + 1) * P], xq[:, j, k, :], eye_b[:])
                last.then_inc(xqt_psum, 1)

            def attend(b):
                pe.wait_ge(xqt_ready, b + 1)
                pe.wait_ge(cq_ready[b], 1)
                if b == 2:
                    pe.wait_ge(logits_copied, 1)
                if b == 3:
                    pe.wait_ge(x1_ready, b)
                for k in range(KC):
                    for jj in range(BT):
                        last = nc.tensor.matmul(ATT[b][k][:, jj * D:(jj + 1) * D], xqt[:, b, k, jj * P:(jj + 1) * P],
                                                cq[:, b, k, :], start=True, stop=True)
                last.then_inc(att_ready, 1)

            def transpose_tokens(b, src, dst, done):
                for k in range(KC):
                    for jj, j in enumerate(tiles(b)):
                        last = nc.tensor.transpose(dst[b][:, k * S + jj * P:k * S + (jj + 1) * P], src[:, j, k * P:(k + 1) * P], eye[:])
                last.then_inc(done, 1)

            def transpose_x1(b):
                pe.wait_ge(x1_ready, b + 1)
                transpose_tokens(b, x1, X1T, x1t_psum)

            def transpose_y2(b):
                pe.wait_ge(y2_ready, b + 1)
                if b == 2:
                    pe.wait_ge(x1_ready, 4)
                if b == 3:
                    pe.wait_ge(x1t_copied, 3)
                transpose_tokens(b, y2, Y2T, y2t_psum)

            def router(h):
                ts = slice(h * HN, (h + 1) * HN)
                pe.wait_ge(gate_split, 1)
                pe.wait_ge(h_lo_done, HB * (h + 1))
                pe.wait_ge(x1t_copied, HB * (h + 1))
                three_passes(LOGIT[h][:], [(gate_hi[:, k, :], gate_lo[:, k, :]) for k in range(KC)],
                             [(h_hi[:, k, ts], h_lo[:, k, ts]) for k in range(KC)], True, True).then_inc(logits_ready, 1)

            def transpose_logits(h):
                pe.wait_ge(logits_copied, h + 1)
                for jj in range(HT):
                    last = nc.tensor.transpose(LOGIT_T[h][:, jj * GP:(jj + 1) * GP], lg_rows[:, jj * P:(jj + 1) * P],
                                               eye[0:GP, 0:GP])
                last.then_inc(logits_t, 1)

            def transpose_comb(h):
                pe.wait_ge(comb_split, h + 1)
                view = combt_view(h)
                for jj in range(HT):
                    last = nc.tensor.transpose(view[:, jj * P:(jj + 1) * P], comb_parts[:, jj, :], eye_b[:])
                last.then_inc(comb_psum, 1)

            def three_passes(out, w, x_of, start, stop):
                blocks = len(w)
                for k in range(blocks):
                    for i, (a, b) in enumerate(((0, 0), (0, 1), (1, 0))):
                        last = nc.tensor.matmul(out, w[k][a], x_of[k][b], start=(start and k == 0 and i == 0),
                                                stop=(stop and k == blocks - 1 and i == 2))
                return last

            def tokens(h):
                ts = slice(h * HN, (h + 1) * HN)
                return [(h_hi[:, k, ts], h_lo[:, k, ts]) for k in range(KC)]

            def w_gu(slot, which):
                at = which * KC * P
                return [(w_hi[:, slot, at + k * P:at + (k + 1) * P], w_lo[:, slot, at + k * P:at + (k + 1) * P])
                        for k in range(KC)]

            def gate(h, n, slot, bank=GATE):
                pe.wait_ge(gu_lo_done, n + 1)
                three_passes(bank[:], w_gu(slot, 0), tokens(h), True, True).then_inc(gate_done, 1)

            def up(h, slot, bank=UP):
                three_passes(bank[:], w_gu(slot, 1), tokens(h), True, True).then_inc(up_done, 1)

            def mix(h, c, rows=P):
                nc.tensor.matmul(MIX[0:rows, :], spread[:, bass.ds(c * P, rows)], comb_t[:, h, :],
                                 start=True, stop=True).then_inc(mix_done, 1)

            def down(n, slot, start=False, stop=False, rows=P):
                pe.wait_ge(d_lo_done, n + 1)
                pe.wait_ge(a_lo_done, n + 1)
                for k in range(KC):
                    ks = slice(GU + k * P, GU + (k + 1) * P)
                    last = three_passes(OUT[k][:], [(w_hi[0:rows, slot, ks], w_lo[0:rows, slot, ks])],
                                        [(a_hi[0:rows, slot, :], a_lo[0:rows, slot, :])], start, stop)
                    if stop:
                        last.then_inc(half_done, 1)

            def products(h, c, s):
                n, slot = UNITS * h + c, (s + h) % 2
                pe.wait_ge(silu_done, n)
                gate(h, n, slot)
                pe.wait_ge(gated_done, n)
                up(h, slot)

            def mix_and_down(h, c, s, start=False):
                n, slot = UNITS * h + c, (s + h) % 2
                pe.wait_ge(act_done, n)
                mix(h, c)
                down(n - 1, 1 - slot, start)

            def unit(h, c, s):
                products(h, c, s)
                mix_and_down(h, c, s)

            def last_unit(h):
                n, slot = UNITS * h + FULL, h % 2
                pe.wait_ge(silu_done, n)
                gate(h, n, slot)
                pe.wait_ge(act_done, n)
                mix(h, FULL, LAST)
                down(n - 1, 1 - slot)

            ctx_block_max(0)
            ctx_scale_rows(0)
            transpose_xq(0)
            attend(0)
            transpose_xq(1)
            attend(1)
            transpose_x1(0)
            transpose_x1(1)
            transpose_y2(0)
            transpose_y2(1)
            router(0)
            gate(0, 0, 0)
            transpose_logits(0)
            up(0, 0)
            gate(0, 1, 1, OUT[0])
            pe.wait_ge(ex_in_ready, 1)
            up(0, 1, OUT[1])
            ctx_block_max(1)
            pe.wait_ge(silu_done, 1)
            gate(0, 2, 0)
            transpose_comb(0)
            pe.wait_ge(sel_landed, 16)
            pe.wait_ge(comb_ready, 1)
            mix(0, 0)
            pe.wait_ge(gated_done, 1)
            up(0, 0)
            pe.wait_ge(act_done, 1)
            mix(0, 1)
            pe.wait_ge(gated_done, 2)
            down(0, 0, start=True)
            mix_and_down(0, 2, 0)
            ctx_scale_rows(1)
            for c in range(3, 7):
                unit(0, c, c % 2)
            transpose_xq(2)
            unit(0, 7, 1)
            transpose_xq(3)
            attend(2)
            unit(0, 8, 0)
            unit(0, 9, 1)
            attend(3)
            unit(0, 10, 0)
            unit(0, 11, 1)
            transpose_x1(2)
            transpose_y2(2)
            unit(0, 12, 0)
            transpose_x1(3)
            products(0, 13, 1)
            transpose_y2(3)
            mix_and_down(0, 13, 1)
            products(0, 14, 0)
            router(1)
            mix_and_down(0, 14, 0)
            transpose_logits(1)
            unit(0, 15, 1)
            last_unit(0)
            pe.wait_ge(gated_done, UNITS)
            gate(1, UNITS, 1)
            up(1, 1)
            transpose_comb(1)
            pe.wait_ge(act_done, UNITS)
            pe.wait_ge(comb_ready, HALVES)
            mix(1, 0)
            down(UNITS - 1, 0, stop=True, rows=LAST)
            products(1, 1, 1)
            pe.wait_ge(act_done, UNITS + 1)
            mix(1, 1)
            pe.wait_ge(fin_done, KC)
            down(UNITS, 1, start=True)
            with pe.Fori(1, FULL // 2) as j:
                unit(1, 2 * j, 0)
                unit(1, 2 * j + 1, 1)
            last_unit(1)
            down(2 * UNITS - 1, 1, stop=True, rows=LAST)


def kernel(**inputs):
    import numpy as np
    import concourse.bacc as bacc
    from concourse.bass_utils import run_bass_kernel_spmd

    a = {k: np.asarray(v) for k, v in inputs.items()}
    xs = np.ascontiguousarray(a["x"].reshape(TILES, P, D).transpose(1, 0, 2))
    ctx_t = np.ascontiguousarray(a["ctx_2048"].reshape(B, D, KC, P).transpose(3, 0, 2, 1))
    gate = np.concatenate([a["L0_ffn_gate_w"], a["L0_ffn_shared_gate_w"], np.zeros((GP - G, D), np.float32)])
    gate_t = np.ascontiguousarray(gate.reshape(GP, KC, P).transpose(2, 1, 0))
    gw = np.concatenate([a["L0_ffn_wg"].reshape(E * EI, D), a["L0_ffn_swg"]])
    uw = np.concatenate([a["L0_ffn_wu"].reshape(E * EI, D), a["L0_ffn_swu"]])
    dw = np.concatenate([a["L0_ffn_wd"].transpose(0, 2, 1).reshape(E * EI, D), a["L0_ffn_swd"].T])

    def cols(w, chunks, rows):
        return w.reshape(chunks, rows, KC, P).transpose(0, 3, 2, 1).reshape(chunks, P, KC * rows)

    cut = FULL * P
    w_full = np.ascontiguousarray(np.concatenate(
        [cols(gw[:cut], FULL, P), cols(uw[:cut], FULL, P), dw[:cut].reshape(FULL, P, D)], axis=2))
    last_d = np.concatenate([dw[cut:], np.zeros((P - LAST, D), np.float32)])
    w_last = np.ascontiguousarray(np.concatenate(
        [cols(np.concatenate([gw[cut:], uw[cut:]]), 1, 2 * LAST)[0], last_d], axis=1))
    owner = np.concatenate([np.repeat(np.arange(E), EI), np.full(SI, E)])
    sel = np.ascontiguousarray(np.tile(np.eye(G, dtype=np.float16)[:, owner], (3, 1)))

    arrays = {"xs": xs, "ctx_t": ctx_t, "g_x": a["g_xattn"], "g_f": a["g_ffn"], "gate_t": gate_t,
              "w_full": w_full, "w_last": w_last, "sel": sel}
    nc = bacc.Bacc("TRN2", target_bir_lowering=False, num_devices=1)
    args = [nc.dram_tensor(n, v.shape, mybir.dt.from_np(v.dtype), kind="ExternalInput").ap() for n, v in arrays.items()]
    out_t = nc.dram_tensor("out_t", (KC, P, T), F32, kind="ExternalOutput").ap()
    flamingo_gated_block(nc, *args, out_t)
    r = run_bass_kernel_spmd(nc, [arrays], core_ids=[0])
    got = r.results[0]["out_t"]
    return np.ascontiguousarray(np.asarray(got).reshape(D, T).T).reshape(B, S, D)
```

```python
from contextlib import ExitStack

import concourse.bass as bass
from concourse import mybir

P = 128
B, S, D = 4, 256, 256
T = B * S
TILES = T // P
HALVES = 2
HT = TILES // HALVES
HN = HT * P
HB = B // HALVES
BT = S // P
KC = D // P
E, TOP = 8, 4
EI, SI = 176, 704
ROWS = E * EI + SI
FULL = ROWS // P
LAST = ROWS - FULL * P
UNITS = FULL + 1
MIXED = E * EI // P + 1
assert E * EI % P == 0
G = E + 1
GP = G + 1
GU = 2 * KC * P
WC = GU + D
GUL = KC * P
LN_EPS = 1e-5
FP8_MAX, ACT_EPS, W_EPS = 448.0, 1e-4, 1e-6
EXP_BITS = 0x7F800000
SUBNORMAL = 2.0 ** -6
MAGIC = 1.5 * 2.0 ** 20

F32, F32R = mybir.dt.float32, mybir.dt.float32r
BF16, F16, I32 = mybir.dt.bfloat16, mybir.dt.float16, mybir.dt.int32
ALU = mybir.AluOpType
ACT = mybir.ActivationFunctionType
AX = mybir.AxisListType


def flamingo_gated_block(nc, xs, ctx_t, g_x, g_f, gate_t, w_full, w_last, sel, out_t):
    with ExitStack() as stack:
        def sb(name, shape, dt=F32):
            return stack.enter_context(nc.sbuf_tensor(name, shape, dt))

        def sem(name):
            return stack.enter_context(nc.semaphore(name))

        x = sb("x", [P, TILES, D])
        xc = sb("xc", [P, TILES, KC, P])
        xe = sb("xe", [P, TILES, KC, P])
        xq = sb("xq", [P, TILES, KC, P], BF16)
        xqt = sb("xqt", [P, B, KC, S], BF16)
        cw = sb("cw", [P, B, KC, 2, P])
        ce = sb("ce", [P, B, KC, 2, P])
        cq = sb("cq", [P, B, KC, 2 * P], BF16)
        x1 = sb("x1", [P, TILES, D])
        y2 = sb("y2", [P, TILES, D])
        x1t = sb("x1t", [P, KC, T])
        h_hi = sb("h_hi", [P, KC, T], F32R)
        h_lo = sb("h_lo", [P, KC, T], F32R)
        bn = sb("bn", [P, 2, TILES, 6])
        mv = sb("mv", [P, 2, TILES, 2])
        ve = sb("ve", [P, 2, TILES])
        rstd = sb("rstd", [P, 2, TILES])
        neg_mean = sb("neg_mean", [P, TILES])
        minus_half = sb("minus_half", [P, TILES])
        amax_x = sb("amax_x", [P, TILES, KC])
        safe_x = sb("safe_x", [P, TILES, KC])
        inv_x = sb("inv_x", [P, TILES, KC])
        mul_x = sb("mul_x", [P, TILES, KC])
        deq_x = sb("deq_x", [P, TILES, KC])
        amax_c = sb("amax_c", [P, HALVES, HB * KC * 2])
        CB = HB * KC * 2
        blk_c = sb("blk_c", [CB, HALVES, 4])
        diag = sb("diag", [CB, HALVES, 2 * CB])
        scl_c = sb("scl_c", [P, HALVES, 2 * CB])
        deq = sb("deq", [P, TILES, KC, 2])
        g_raw = sb("g_raw", [P, 2])
        g_tanh = sb("g_tanh", [P, 2])
        gate_raw = sb("gate_raw", [P, KC, P])
        gate_hi = sb("gate_hi", [P, KC, P], F32R)
        gate_lo = sb("gate_lo", [P, KC, P], F32R)
        lg_rows = sb("lg_rows", [GP, HN])
        lg = sb("lg", [P, HT, GP])
        lmax = sb("lmax", [P, HT])
        ex_in = sb("ex_in", [P, HT, G])
        ex = sb("ex", [P, HT, G])
        gt = sb("gt", [P, HT, E, E])
        eq = sb("eq", [P, HT, E, E])
        before = sb("before", [P, E, E])
        rank = sb("rank", [P, HT, E])
        wsum = sb("wsum", [P, HT, 2])
        comb = sb("comb", [P, HT, G])
        rest = sb("rest", [P, HT, G])
        comb_parts = sb("comb_parts", [P, HT, P], BF16)
        comb_t = sb("comb_t", [P, HALVES, HN], BF16)
        spread = sb("spread", [P, UNITS * P], F16)
        w_raw = sb("w_raw", [P, UNITS, WC])
        w_hi = sb("w_hi", [P, 2, WC], F32R)
        w_lo = sb("w_lo", [P, 2, WC], F32R)
        silu = sb("silu", [P, 2, HN])
        act = sb("act", [P, 2, HN])
        a_hi = sb("a_hi", [P, 2, HN], F32R)
        a_lo = sb("a_lo", [P, 2, HN], F32R)
        fin = sb("fin", [P, 2, HN])
        eye = sb("eye", [P, P])
        eye_b = sb("eye_b", [P, P], BF16)
        ones = sb("ones", [CB, P])

        bank = [stack.enter_context(nc.psum_tensor(f"bank{i}", [P, HN], F32)) for i in range(8)]
        GATE, UP, MIX = bank[0:3]
        OUT = (bank[3:5], bank[6:8])
        GATE_LAST = bank[5]
        QT = [bank[i] for i in (0, 1, 5, 7)]
        ATT = [[bank[i] for i in ks] for ks in ((2, 3), (4, 5), (6, 5), (7, 5))]
        X1T = [bank[i] for i in (6, 2, 6, 7)]
        Y2T = [bank[i] for i in (7, 3, 6, 5)]
        BLK, LOGIT, LOGIT_T, COMBT = ((bank[i], bank[j]) for i, j in ((7, 5), (6, 7), (4, 5), (7, 6)))

        x_landed = [sem(f"x_landed{b}") for b in range(B)]
        ctx_landed = [sem(f"ctx_landed{h}") for h in range(HALVES)]
        gates_landed = sem("gates_landed")
        gate_w_landed = sem("gate_w_landed")
        sel_landed = sem("sel_landed")
        w_landed = [sem(f"w_landed{i}") for i in range(2)]
        stored = sem("stored")
        consts, ident_filled = sem("consts"), sem("ident_filled")
        gate_zeroed, spread_zeroed = sem("gate_zeroed"), sem("spread_zeroed")
        tanh_done, gate_hi_done, gate_split = sem("tanh_done"), sem("gate_hi_done"), sem("gate_split")
        dve_did, pool_did = sem("dve_did"), sem("pool_did")
        ctx_amax, ctx_amax_t, ctx_diag = sem("ctx_amax"), sem("ctx_amax_t"), sem("ctx_diag")
        ctx_scales, ctx_scales_copied = sem("ctx_scales"), sem("ctx_scales_copied")
        ctx_scaled, ctx_magic = sem("ctx_scaled"), sem("ctx_magic")
        cq_ready = [sem(f"cq_ready{b}") for b in range(B)]
        deq_ready = sem("deq_ready")
        logits_ready, ex_in_ready, ex_ready = sem("logits_ready"), sem("ex_in_ready"), sem("ex_ready")
        logits_copied, logits_t = sem("logits_copied"), sem("logits_t")
        comb_split, comb_psum, comb_ready = sem("comb_split"), sem("comb_psum"), sem("comb_ready")
        var_ready, rstd_ready, centred = sem("var_ready"), sem("rstd_ready"), sem("centred")
        mul_x_ready, x_scaled = sem("mul_x_ready"), sem("x_scaled")
        xq_ready, xqt_psum, xqt_ready = sem("xq_ready"), sem("xqt_psum"), sem("xqt_ready")
        att_ready, res0_ready = sem("att_ready"), sem("res0_ready")
        part0_done, y2_ready = sem("part0_done"), sem("y2_ready")
        x1_ready = [sem(f"x1_ready{b}") for b in range(B)]
        var1_ready, rstd1_ready = sem("var1_ready"), sem("rstd1_ready")
        x1t_psum, x1t_copied = sem("x1t_psum"), sem("x1t_copied")
        y2t_psum, h_hi_done, h_lo_done = sem("y2t_psum"), sem("h_hi_done"), sem("h_lo_done")
        gu_hi_done, gu_lo_done = sem("gu_hi_done"), sem("gu_lo_done")
        d_hi_done, d_lo_done = sem("d_hi_done"), sem("d_lo_done")
        gate_done, up_done, mix_done, silu_done = sem("gate_done"), sem("up_done"), sem("mix_done"), sem("silu_done")
        gated_done, act_done, a_hi_done, a_lo_done = sem("gated_done"), sem("act_done"), sem("a_hi_done"), sem("a_lo_done")
        half_done, fin_done, down_slot_free = sem("half_done"), sem("fin_done"), sem("down_slot_free")

        def tiles(b):
            return range(BT * b, BT * (b + 1))

        def tile_slice(b):
            return slice(BT * b, BT * (b + 1))

        def batches(h):
            return slice(HB * h, HB * (h + 1))

        def qt_view(b):
            return QT[b][:].bitcast(BF16)[:, 0:KC * S].rearrange("p (k t) -> p k t", k=KC)

        def combt_view(h):
            return COMBT[h][:].bitcast(BF16)[:, 0:HN]

        block = stack.enter_context(nc.Block())

        @block.sync
        def _(sp):
            def load_x(b):
                sp.dma_start(x[:, tile_slice(b), :], xs[:, tile_slice(b), :]).then_inc(x_landed[b], 16)

            load_x(0)
            load_x(1)
            sp.wait_ge(gate_zeroed, 1)
            sp.dma_start(gate_raw[:, :, 0:GP], gate_t).then_inc(gate_w_landed, 16)
            sp.dma_start(g_raw[:, 0:1], g_x.to_broadcast((P, 1))).then_inc(gates_landed, 16)
            sp.dma_start(g_raw[:, 1:2], g_f.to_broadcast((P, 1))).then_inc(gates_landed, 16)
            load_x(2)
            load_x(3)
            sp.dma_start(cw[:, batches(1)], ctx_t[:, batches(1)]).then_inc(ctx_landed[1], 16)
            sp.wait_ge(spread_zeroed, 1)
            sp.dma_start(spread[0:3 * G, 0:ROWS], sel).then_inc(sel_landed, 16)
            for c in range(UNITS):
                if c >= 2:
                    sp.wait_ge(w_landed[c % 2], 16 * (c // 2))
                if c < FULL:
                    sp.dma_start(w_raw[:, c, :], w_full[c]).then_inc(w_landed[c % 2], 16)
                else:
                    sp.dma_start(w_raw[:, c, 0:GUL + D], w_last).then_inc(w_landed[c % 2], 16)
            for n in range(HALVES * KC):
                h, k = n // KC, n % KC
                sp.wait_ge(fin_done, n + 1)
                sp.dma_start(out_t[k, :, h * HN:(h + 1) * HN], fin[:, k, :]).then_inc(stored, 16)
            sp.wait_ge(stored, 16 * HALVES * KC)

        @block.gpsimd
        def _(pool):
            nc.gpsimd.memzero(gate_raw[:]).then_inc(gate_zeroed, 1)
            nc.gpsimd.memset(eye[:], 0.0).then_inc(ident_filled, 1)
            nc.gpsimd.memset(minus_half[:], -0.5)
            nc.gpsimd.memset(ones[:], 1.0)
            pool.wait_ge(ident_filled, 1)
            nc.gpsimd.affine_select(out=eye[:], in_=eye[:], compare_op=ALU.not_equal, fill=1.0, base=0,
                                    pattern=[[-1, P]], channel_multiplier=1).then_inc(ident_filled, 1)
            nc.gpsimd.memset(before[:], 0.0).then_inc(ident_filled, 1)
            pool.wait_ge(ident_filled, 3)
            nc.gpsimd.affine_select(out=before[:], in_=before[:], compare_op=ALU.is_ge, fill=1.0, base=0,
                                    pattern=[[-1, E], [1, E]], channel_multiplier=0)
            nc.gpsimd.tensor_copy(eye_b[:], eye[:])
            nc.gpsimd.memzero(comb_parts[:]).then_inc(consts, 1)
            nc.gpsimd.memzero(spread[:]).then_inc(spread_zeroed, 1)

            def inverse_std(which, b, var_sem, rstd_sem):
                pool.wait_ge(var_sem, b + 1)
                nc.gpsimd.tensor_tensor(rstd[:, which, tile_slice(b)], ve[:, which, tile_slice(b)],
                                        minus_half[:, 0:BT], ALU.pow).then_inc(rstd_sem, 1)

            def add_magic(b):
                pool.wait_ge(ctx_magic, b + 1)
                val = cw[:, b].rearrange("p k n c -> p (k n c)")
                nc.gpsimd.tensor_tensor(val, val, ce[:, b].rearrange("p k n c -> p (k n c)"), ALU.add).then_inc(pool_did, 1)

            def subtract_magic(b):
                pool.wait_ge(pool_did, b + 1)
                nc.gpsimd.tensor_tensor(cq[:, b].rearrange("p k c -> p (k c)"), cw[:, b].rearrange("p k n c -> p (k n c)"),
                                        ce[:, b].rearrange("p k n c -> p (k n c)"), ALU.subtract).then_inc(cq_ready[b], 1)

            def residual_sum_0():
                pool.wait_ge(part0_done, 1)
                pool.wait_ge(res0_ready, 1)
                nc.gpsimd.tensor_tensor(x1[:, tile_slice(0), :], x1[:, tile_slice(0), :], y2[:, tile_slice(0), :], ALU.add)\
                    .then_inc(x1_ready[0], 1)

            def low_gu(n, c, slot, cols=GU):
                pool.wait_ge(gu_hi_done, n + 1)
                nc.gpsimd.tensor_tensor(w_lo[:, slot, 0:cols], w_raw[:, bass.ds(c, 1), 0:cols],
                                        w_hi[:, slot, 0:cols].bitcast(F32), ALU.subtract).then_inc(gu_lo_done, 1)

            def low_d(n, c, slot, rows=P, at=GU):
                pool.wait_ge(d_hi_done, n + 1)
                nc.gpsimd.tensor_tensor(w_lo[0:rows, slot, GU:WC], w_raw[0:rows, bass.ds(c, 1), at:at + D],
                                        w_hi[0:rows, slot, GU:WC].bitcast(F32), ALU.subtract).then_inc(d_lo_done, 1)

            def unit(h, c, s):
                n, slot = UNITS * h + c, (s + h) % 2
                low_gu(n + 1, c + 1, 1 - slot)
                low_d(n, c, slot)

            inverse_std(0, 0, var_ready, rstd_ready)
            inverse_std(0, 1, var_ready, rstd_ready)
            add_magic(0)
            subtract_magic(0)
            add_magic(1)
            subtract_magic(1)
            residual_sum_0()
            inverse_std(1, 0, var1_ready, rstd1_ready)
            inverse_std(1, 1, var1_ready, rstd1_ready)
            low_gu(0, 0, 0)
            inverse_std(0, 2, var_ready, rstd_ready)
            unit(0, 0, 0)
            unit(0, 1, 1)
            unit(0, 2, 0)
            inverse_std(0, 3, var_ready, rstd_ready)
            for c in range(3, 6):
                unit(0, c, c % 2)
            add_magic(2)
            unit(0, 6, 0)
            subtract_magic(2)
            add_magic(3)
            unit(0, 7, 1)
            subtract_magic(3)
            for c in range(8, 11):
                unit(0, c, c % 2)
            inverse_std(1, 2, var1_ready, rstd1_ready)
            unit(0, 11, 1)
            unit(0, 12, 0)
            inverse_std(1, 3, var1_ready, rstd1_ready)
            unit(0, 13, 1)
            unit(0, FULL - 2, 0)
            low_gu(FULL, FULL, 0, GUL)
            low_d(FULL - 1, FULL - 1, 1)
            low_gu(UNITS, 0, 1)
            low_d(FULL, FULL, 0, LAST, GUL)
            with pool.Fori(0, FULL // 2 - 1) as j:
                unit(1, 2 * j, 0)
                unit(1, 2 * j + 1, 1)
            last_n = 2 * UNITS - 1
            low_gu(last_n - 1, FULL, 0, GUL)
            low_d(last_n - 2, FULL - 2, 1)
            low_gu(last_n, FULL - 1, 1)
            low_d(last_n - 1, FULL, 0, LAST, GUL)
            low_d(last_n, FULL - 1, 1)

        @block.scalar
        def _(a):
            a.dma_start(cw[:, batches(0)], ctx_t[:, batches(0)]).then_inc(ctx_landed[0], 16)
            a.preload_act_table(ACT.Exp)

            def centre(b):
                a.wait_ge(var_ready, b + 1)
                for j in tiles(b):
                    last = nc.scalar.activation(xc[:, j].rearrange("p k c -> p (k c)"), x[:, j, :], ACT.Identity,
                                                bias=neg_mean[:, j:j + 1])
                last.then_inc(centred, 1)

            def scale_ctx(b):
                h, per = b // HB, 2 * KC
                a.wait_ge(ctx_scales_copied, h + 1)
                for i in range(per):
                    at = (b % HB) * per + i
                    last = nc.scalar.activation(cw[:, b, i // 2, i % 2, :], cw[:, b, i // 2, i % 2, :], ACT.Copy,
                                                scale=scl_c[:, h, at:at + 1])
                last.then_inc(ctx_scaled, 1)

            def scale_x(b):
                a.wait_ge(mul_x_ready, b + 1)
                for j in tiles(b):
                    for k in range(KC):
                        last = nc.scalar.activation(xc[:, j, k, :], xc[:, j, k, :], ACT.Copy,
                                                    scale=mul_x[:, j, k:k + 1])
                last.then_inc(x_scaled, 1)

            def copy_xqt(b):
                a.wait_ge(xqt_psum, b + 1)
                nc.scalar.activation(xqt[:, b], qt_view(b), ACT.Copy).then_inc(xqt_ready, 1)

            def residual0(b):
                a.wait_ge(att_ready, b + 1)
                a.wait_ge(deq_ready, b // HB + 1)
                for jj, j in enumerate(tiles(b)):
                    for n in range(2):
                        last = nc.scalar.activation(y2[:, j, n * P:(n + 1) * P], ATT[b][0][:, jj * D + n * P:jj * D + (n + 1) * P],
                                                    ACT.Copy, scale=deq[:, j, 0, n:n + 1])
                last.then_inc(res0_ready, 1)

            def copy_x1t(b):
                a.wait_ge(x1t_psum, b + 1)
                nc.scalar.activation(x1t[:, :, b * S:(b + 1) * S], X1T[b][:].rearrange("p (k t) -> p k t", k=KC), ACT.Copy)\
                    .then_inc(x1t_copied, 1)

            def high_h(b):
                a.wait_ge(y2t_psum, b + 1)
                nc.scalar.activation(h_hi[:, :, b * S:(b + 1) * S], Y2T[b][:].rearrange("p (k t) -> p k t", k=KC), ACT.Copy)\
                    .then_inc(h_hi_done, 1)

            def copy_logits(h):
                a.wait_ge(logits_ready, h + 1)
                nc.scalar.activation(lg_rows[:], LOGIT[h][0:GP, :], ACT.Copy).then_inc(logits_copied, 1)

            def exp_router(h):
                a.wait_ge(ex_in_ready, h + 1)
                nc.scalar.activation(ex[:], ex_in[:], ACT.Exp).then_inc(ex_ready, 1)

            def copy_comb(h):
                a.wait_ge(comb_psum, h + 1)
                nc.scalar.activation(comb_t[:, h], combt_view(h), ACT.Copy).then_inc(comb_ready, 1)

            def high_gu(c, slot, ups, cols=GU):
                if ups is not None:
                    a.wait_ge(up_done, ups)
                nc.scalar.activation(w_hi[:, slot, 0:cols], w_raw[:, bass.ds(c, 1), 0:cols], ACT.Copy)\
                    .then_inc(gu_hi_done, 1)

            def high_d(c, slot, rows=P, at=GU):
                nc.scalar.activation(w_hi[0:rows, slot, GU:WC], w_raw[0:rows, bass.ds(c, 1), at:at + D], ACT.Copy)\
                    .then_inc(d_hi_done, 1)

            def silu_unit(n, slot, rows=P, bank=GATE):
                a.wait_ge(gate_done, n + 1)
                nc.scalar.activation(silu[0:rows, slot, :], bank[0:rows, :], ACT.Silu).then_inc(silu_done, 1)

            def high_a(n, slot, rows=P):
                a.wait_ge(act_done, n + 1)
                nc.scalar.activation(a_hi[0:rows, slot, :], act[0:rows, slot, :], ACT.Copy).then_inc(a_hi_done, 1)

            def weights(h, c, s, first=False, cols=GU):
                if h == 0:
                    a.wait_ge(w_landed[s], 16 * (c // 2 + 1))
                high_gu(c, (s + h) % 2, None if first else FULL * h + c - 1, cols)

            def silu_and_down(h, c, s):
                silu_unit(UNITS * h + c, (s + h) % 2)
                high_d(c, (s + h) % 2)

            def unit(h, c, s):
                weights(h, c + 1, 1 - s)
                silu_and_down(h, c, s)
                high_a(UNITS * h + c, (s + h) % 2)

            centre(0)
            scale_ctx(0)
            scale_x(0)
            centre(1)
            scale_ctx(1)
            a.wait_ge(gates_landed, 32)
            nc.scalar.activation(g_tanh[:], g_raw[:], ACT.Tanh).then_inc(tanh_done, 1)
            scale_x(1)
            copy_xqt(0)
            copy_xqt(1)
            residual0(0)
            a.wait_ge(gate_w_landed, 16)
            nc.scalar.activation(gate_hi[:], gate_raw[:], ACT.Copy).then_inc(gate_hi_done, 1)
            weights(0, 0, 0, first=True)
            residual0(1)
            copy_x1t(0)
            copy_x1t(1)
            high_h(0)
            high_h(1)
            weights(0, 1, 1, first=True)
            high_d(0, 0)
            copy_logits(0)
            centre(2)
            exp_router(0)
            weights(0, 2, 0)
            silu_unit(0, 0)
            silu_unit(1, 1, bank=OUT[0][0])
            copy_comb(0)
            high_d(1, 1)
            high_a(0, 0)
            weights(0, 3, 1)
            silu_unit(2, 0)
            high_a(1, 1)
            a.wait_ge(mix_done, 3)
            high_d(2, 0)
            high_a(2, 0)
            weights(0, 4, 0)
            centre(3)
            silu_and_down(0, 3, 1)
            scale_x(2)
            high_a(3, 1)
            weights(0, 5, 1)
            scale_ctx(2)
            silu_and_down(0, 4, 0)
            scale_x(3)
            high_a(4, 0)
            weights(0, 6, 0)
            scale_ctx(3)
            silu_and_down(0, 5, 1)
            high_a(5, 1)
            unit(0, 6, 0)
            weights(0, 8, 0)
            copy_xqt(2)
            silu_and_down(0, 7, 1)
            high_a(7, 1)
            weights(0, 9, 1)
            silu_and_down(0, 8, 0)
            copy_xqt(3)
            residual0(2)
            high_a(8, 0)
            unit(0, 9, 1)
            weights(0, 11, 1)
            silu_and_down(0, 10, 0)
            residual0(3)
            high_a(10, 0)
            weights(0, 12, 0)
            copy_x1t(2)
            silu_and_down(0, 11, 1)
            high_a(11, 1)
            weights(0, 13, 1)
            high_h(2)
            silu_and_down(0, 12, 0)
            high_a(12, 0)
            weights(0, 14, 0)
            copy_x1t(3)
            silu_and_down(0, 13, 1)
            high_h(3)
            high_a(13, 1)
            weights(0, 15, 1)
            silu_and_down(0, 14, 0)
            copy_logits(1)
            high_a(14, 0)
            weights(0, FULL, 0, cols=GUL)
            silu_and_down(0, FULL - 1, 1)
            exp_router(1)
            high_gu(0, 1, FULL)
            high_a(FULL - 1, 1)
            silu_unit(FULL, 0, LAST)
            high_d(FULL, 0, LAST, GUL)
            weights(1, 1, 1)
            high_a(FULL, 0, LAST)
            silu_unit(UNITS, 1, bank=LOGIT[1])
            copy_comb(1)
            high_d(0, 1)
            high_a(UNITS, 1)
            unit(1, 1, 1)
            with a.Fori(1, FULL // 2 - 1) as j:
                unit(1, 2 * j, 0)
                unit(1, 2 * j + 1, 1)
            last_n = 2 * UNITS - 1
            high_gu(FULL, 0, HALVES * FULL - 2, GUL)
            silu_and_down(1, FULL - 2, 0)
            high_gu(FULL - 1, 1, HALVES * FULL - 1)
            high_a(last_n - 2, 1)
            silu_unit(last_n - 1, 0, LAST, GATE_LAST)
            high_d(FULL, 0, LAST, GUL)
            silu_unit(last_n, 1)
            high_a(last_n - 1, 0, LAST)
            a.wait_ge(down_slot_free, 1)
            high_d(FULL - 1, 1)
            high_a(last_n, 1)

        @block.vector
        def _(v):
            steps = [0]

            def did(ins):
                steps[0] += 1
                ins.then_inc(dve_did, 1)
                return steps[0]

            def after(step):
                v.wait_ge(dve_did, step)

            def max_ctx(h):
                v.wait_ge(ctx_landed[h], 16)
                nc.vector.tensor_reduce(amax_c[:, h, :], cw[:, batches(h)].rearrange("p b k n c -> p (b k n) c"),
                                        op=ALU.max, axis=AX.X, apply_absolute_value=True).then_inc(ctx_amax, 1)

            def stats(which, src, b):
                for j in tiles(b):
                    last = nc.vector.bn_stats(bn[:, which, j, :], src[:, j, :])
                after(did(last))
                for j in tiles(b):
                    last = nc.vector.bn_aggr(mv[:, which, j, :], bn[:, which, j, :])
                after(did(last))
                if which == 0:
                    nc.vector.tensor_scalar(neg_mean[:, tile_slice(b)], mv[:, 0, tile_slice(b), 0], -1.0, None, ALU.mult)
                return nc.vector.tensor_scalar(ve[:, which, tile_slice(b)], mv[:, which, tile_slice(b), 1],
                                               LN_EPS, None, ALU.add)

            def stats_x(b):
                v.wait_ge(x_landed[b], 16)
                stats(0, x, b).then_inc(var_ready, 1)

            def block_scales_ctx(h):
                v.wait_ge(ctx_amax_t, h + 1)
                after(did(nc.vector.tensor_reduce(blk_c[:, h, 0:1], BLK[h][0:CB, 0:P], op=ALU.max, axis=AX.X)))
                after(did(nc.vector.tensor_scalar(blk_c[:, h, 1:2], blk_c[:, h, 0:1], W_EPS, None, ALU.max)))
                after(did(nc.vector.reciprocal(blk_c[:, h, 2:3], blk_c[:, h, 1:2])))
                nc.vector.tensor_scalar(diag[:, h, 0:CB], eye[0:CB, 0:CB], blk_c[:, h, 2:3], FP8_MAX, ALU.mult, ALU.mult)
                nc.vector.tensor_scalar(diag[:, h, CB:2 * CB], eye[0:CB, 0:CB], blk_c[:, h, 1:2], 1.0 / FP8_MAX,
                                        ALU.mult, ALU.mult).then_inc(ctx_diag, 1)

            def copy_scales_ctx(h):
                v.wait_ge(ctx_scales, h + 1)
                nc.vector.tensor_copy(scl_c[:, h, :], BLK[h][:, P:P + 2 * CB]).then_inc(ctx_scales_copied, 1)

            def exponents(mag, val):
                return nc.vector.tensor_scalar(mag.bitcast(I32), val.bitcast(I32), EXP_BITS, None, ALU.bitwise_and)

            def exponents_ctx(b):
                v.wait_ge(ctx_scaled, b + 1)
                return did(exponents(ce[:, b].rearrange("p k n c -> p (k n c)"), cw[:, b].rearrange("p k n c -> p (k n c)")))

            def magic_ctx(b, exponents_step):
                after(exponents_step)
                mag = ce[:, b].rearrange("p k n c -> p (k n c)")
                nc.vector.tensor_scalar(mag, mag, SUBNORMAL, MAGIC, ALU.max, ALU.mult).then_inc(ctx_magic, 1)

            def max_x(b):
                v.wait_ge(centred, b + 1)
                return did(nc.vector.tensor_reduce(amax_x[:, tile_slice(b), :], xc[:, tile_slice(b)],
                                                   op=ALU.max, axis=AX.X, apply_absolute_value=True))

            def scales_x(b, amax_step):
                js = tile_slice(b)
                r = rstd[:, 0, js].unsqueeze(2).to_broadcast((P, BT, KC))
                v.wait_ge(rstd_ready, b + 1)
                after(amax_step)
                after(did(nc.vector.tensor_tensor(safe_x[:, js], amax_x[:, js], r, ALU.mult)))
                after(did(nc.vector.tensor_scalar(safe_x[:, js], safe_x[:, js], ACT_EPS, None, ALU.max)))
                after(did(nc.vector.reciprocal(inv_x[:, js], safe_x[:, js])))
                nc.vector.scalar_tensor_tensor(mul_x[:, js], inv_x[:, js], FP8_MAX, r, ALU.mult, ALU.mult)\
                    .then_inc(mul_x_ready, 1)

            def exponents_x(b):
                v.wait_ge(x_scaled, b + 1)
                flat = "p j k c -> p (j k c)"
                return did(exponents(xe[:, tile_slice(b)].rearrange(flat), xc[:, tile_slice(b)].rearrange(flat)))

            def magic_x(b, exponents_step):
                after(exponents_step)
                mag = xe[:, tile_slice(b)].rearrange("p j k c -> p (j k c)")
                return did(nc.vector.tensor_scalar(mag, mag, SUBNORMAL, MAGIC, ALU.max, ALU.mult))

            def round_x(b, magic_step):
                flat = "p j k c -> p (j k c)"
                val, mag = xc[:, tile_slice(b)].rearrange(flat), xe[:, tile_slice(b)].rearrange(flat)
                after(magic_step)
                after(did(nc.vector.tensor_tensor(val, val, mag, ALU.add)))
                nc.vector.tensor_tensor(xq[:, tile_slice(b)].rearrange(flat), val, mag, ALU.subtract).then_inc(xq_ready, 1)

            def dequant_scales(h):
                js, by_batch = slice(HT * h, HT * (h + 1)), (P, HB, BT, 2)
                back = scl_c[:, h, CB:2 * CB].rearrange("p (b k n) -> p b k n", b=HB, k=KC)
                v.wait_ge(tanh_done, 1)
                after(did(nc.vector.tensor_scalar(deq_x[:, js], safe_x[:, js], 1.0 / FP8_MAX, g_tanh[:, 0:1],
                                                  ALU.mult, ALU.mult)))
                for k in range(KC):
                    last = nc.vector.tensor_tensor(
                        deq[:, js, k, :].rearrange("p (b j) n -> p b j n", b=HB),
                        deq_x[:, js, k].rearrange("p (b j) -> p b j", b=HB).unsqueeze(3).to_broadcast(by_batch),
                        back[:, :, k, :].unsqueeze(2).to_broadcast(by_batch), ALU.mult)
                last.then_inc(deq_ready, 1)

            def residual1(b):
                v.wait_ge(att_ready, b + 1)
                v.wait_ge(deq_ready, b // HB + 1)
                for jj, j in enumerate(tiles(b)):
                    for n in range(2):
                        ns = slice(n * P, (n + 1) * P)
                        last = nc.vector.scalar_tensor_tensor(x1[:, j, ns], ATT[b][1][:, jj * D + n * P:jj * D + (n + 1) * P],
                                                              deq[:, j, 1, n:n + 1], x[:, j, ns], ALU.mult, ALU.add)
                if b == 0:
                    last.then_inc(part0_done, 1)
                    return None
                return did(last)

            def residual_sum(b, step):
                after(step)
                v.wait_ge(res0_ready, b + 1)
                nc.vector.tensor_tensor(x1[:, tile_slice(b), :], x1[:, tile_slice(b), :], y2[:, tile_slice(b), :], ALU.add)\
                    .then_inc(x1_ready[b], 1)

            def stats_x1(b):
                v.wait_ge(x1_ready[b], 1)
                stats(1, x1, b).then_inc(var1_ready, 1)

            def norm_x1(b):
                v.wait_ge(rstd1_ready, b + 1)
                for j in tiles(b):
                    last = nc.vector.tensor_scalar(y2[:, j, :], x1[:, j, :], mv[:, 1, j, 0:1], rstd[:, 1, j:j + 1],
                                                   ALU.subtract, ALU.mult)
                last.then_inc(y2_ready, 1)

            def low_h(b):
                ts = slice(b * S, (b + 1) * S)
                v.wait_ge(h_hi_done, b + 1)
                nc.vector.tensor_tensor(h_lo[:, :, ts], Y2T[b][:].rearrange("p (k t) -> p k t", k=KC),
                                        h_hi[:, :, ts].bitcast(F32), ALU.subtract).then_inc(h_lo_done, 1)

            def split_gate_w():
                v.wait_ge(gate_hi_done, 1)
                nc.vector.tensor_tensor(gate_lo[:], gate_raw[:], gate_hi[:].bitcast(F32), ALU.subtract)\
                    .then_inc(gate_split, 1)

            def route_compare(h):
                v.wait_ge(logits_t, h + 1)
                after(did(nc.vector.tensor_copy(lg[:], LOGIT_T[h][:, 0:HT * GP].rearrange("p (j g) -> p j g", j=HT))))
                l = lg[:, :, 0:E]
                li = l.unsqueeze(3).to_broadcast((P, HT, E, E))
                lj = l.unsqueeze(2).to_broadcast((P, HT, E, E))
                maxed = did(nc.vector.tensor_reduce(lmax[:], l, op=ALU.max, axis=AX.X))
                equal = did(nc.vector.tensor_tensor(eq[:], lj, li, ALU.is_equal))
                nc.vector.tensor_tensor(gt[:], lj, li, ALU.is_gt)
                after(maxed)
                nc.vector.tensor_tensor(ex_in[:, :, 0:E], l, lmax[:].unsqueeze(2).to_broadcast((P, HT, E)), ALU.subtract)
                nc.vector.tensor_scalar(ex_in[:, :, E:G], lg[:, :, E:G], -1.0, None, ALU.mult).then_inc(ex_in_ready, 1)
                return equal

            def route_rank(equal):
                after(equal)
                after(did(nc.vector.tensor_tensor(eq[:], eq[:], before[:].unsqueeze(1).to_broadcast((P, HT, E, E)), ALU.mult)))
                after(did(nc.vector.tensor_tensor(gt[:], gt[:], eq[:], ALU.add)))
                return did(nc.vector.tensor_reduce(rank[:], gt[:], op=ALU.add, axis=AX.X))

            def route_weigh(h, ranked):
                after(ranked)
                v.wait_ge(ex_ready, h + 1)
                chosen = did(nc.vector.scalar_tensor_tensor(comb[:, :, 0:E], rank[:], TOP - 0.5, ex[:, :, 0:E], ALU.is_lt, ALU.mult))
                nc.vector.tensor_scalar(wsum[:, :, 1], ex[:, :, E], 1.0, None, ALU.add)
                after(chosen)
                after(did(nc.vector.tensor_reduce(wsum[:, :, 0:1], comb[:, :, 0:E], op=ALU.add, axis=AX.X)))
                after(did(nc.vector.reciprocal(wsum[:], wsum[:])))
                nc.vector.tensor_tensor(comb[:, :, 0:E], comb[:, :, 0:E], wsum[:, :, 0:1].to_broadcast((P, HT, E)), ALU.mult)
                after(did(nc.vector.tensor_copy(comb[:, :, E:G], wsum[:, :, 1:2])))
                if h >= 1:
                    v.wait_ge(comb_psum, h)
                after(did(nc.vector.tensor_copy(comb_parts[:, :, 0:G], comb[:])))
                nc.vector.tensor_tensor(rest[:], comb[:], comb_parts[:, :, 0:G], ALU.subtract)
                after(did(nc.vector.tensor_tensor(comb_parts[:, :, G:2 * G], comb[:], comb_parts[:, :, 0:G], ALU.subtract)))
                nc.vector.tensor_tensor(comb_parts[:, :, 2 * G:3 * G], rest[:], comb_parts[:, :, G:2 * G], ALU.subtract)\
                    .then_inc(comb_split, 1)

            def gated(n, slot, up, ups, rows=P):
                v.wait_ge(silu_done, n + 1)
                if ups is not None:
                    v.wait_ge(up_done, ups)
                nc.vector.tensor_tensor(silu[0:rows, slot, :], silu[0:rows, slot, :], up, ALU.mult).then_inc(gated_done, 1)

            def mixed(n, slot, mixes=None, rows=P):
                v.wait_ge(gated_done, n + 1)
                if mixes is not None:
                    v.wait_ge(mix_done, mixes)
                nc.vector.tensor_tensor(act[0:rows, slot, :], silu[0:rows, slot, :], MIX[0:rows, :], ALU.mult)\
                    .then_inc(act_done, 1)

            def low_a(n, slot, rows=P):
                v.wait_ge(a_hi_done, n + 1)
                nc.vector.tensor_tensor(a_lo[0:rows, slot, :], act[0:rows, slot, :], a_hi[0:rows, slot, :].bitcast(F32),
                                        ALU.subtract).then_inc(a_lo_done, 1)

            def unit(h, c, s, own_mix=True):
                n, slot = UNITS * h + c, (s + h) % 2
                gated(n, slot, UP[:], FULL * h + c + 1)
                mixed(n, slot, MIXED * h + c + 1 if own_mix else None)
                low_a(n, slot)

            def finish(h):
                for k in range(KC):
                    v.wait_ge(half_done, KC * h + k + 1)
                    if h >= 1:
                        v.wait_ge(stored, 16 * KC * h)
                    nc.vector.scalar_tensor_tensor(fin[:, k, :], OUT[h][k][:], g_tanh[:, 1:2], x1t[:, k, h * HN:(h + 1) * HN],
                                                   ALU.mult, ALU.add).then_inc(fin_done, 1)

            stats_x(0)
            max_ctx(0)
            max_x_0 = max_x(0)
            v.wait_ge(consts, 1)
            block_scales_ctx(0)
            scales_x(0, max_x_0)
            copy_scales_ctx(0)
            stats_x(1)
            magic_ctx(0, exponents_ctx(0))
            magic_0 = magic_x(0, exponents_x(0))
            scales_x(1, max_x(1))
            round_x(0, magic_0)
            exp_ctx, exp_x = exponents_ctx(1), exponents_x(1)
            magic_ctx(1, exp_ctx)
            round_x(1, magic_x(1, exp_x))
            dequant_scales(0)
            residual1(0)
            part_1 = residual1(1)
            stats_x1(0)
            residual_sum(1, part_1)
            norm_x1(0)
            stats_x1(1)
            split_gate_w()
            norm_x1(1)
            low_h(0)
            low_h(1)
            stats_x(2)
            max_ctx(1)
            route_weigh(0, route_rank(route_compare(0)))
            gated(0, 0, UP[:], 1)
            gated(1, 1, OUT[0][1][:], 2)
            mixed(0, 0, 1)
            stats_x(3)
            low_a(0, 0)
            mixed(1, 1, 2)
            low_a(1, 1)
            block_scales_ctx(1)
            unit(0, 2, 0)
            copy_scales_ctx(1)
            scales_x(2, max_x(2))
            unit(0, 3, 1)
            scales_x(3, max_x(3))
            unit(0, 4, 0)
            exp_ctx, exp_x = exponents_ctx(2), exponents_x(2)
            magic_ctx(2, exp_ctx)
            magic_2 = magic_x(2, exp_x)
            unit(0, 5, 1)
            round_x(2, magic_2)
            magic_ctx(3, exponents_ctx(3))
            unit(0, 6, 0)
            round_x(3, magic_x(3, exponents_x(3)))
            unit(0, 7, 1)
            dequant_scales(1)
            unit(0, 8, 0)
            part_2 = residual1(2)
            unit(0, 9, 1)
            residual_sum(2, part_2)
            stats_x1(2)
            unit(0, 10, 0)
            norm_x1(2)
            part_3 = residual1(3)
            unit(0, 11, 1)
            residual_sum(3, part_3)
            stats_x1(3)
            unit(0, 12, 0, own_mix=False)
            norm_x1(3)
            low_h(2)
            unit(0, 13, 1, own_mix=False)
            low_h(3)
            unit(0, 14, 0, own_mix=False)
            ranked = route_rank(route_compare(1))
            unit(0, 15, 1, own_mix=False)
            route_weigh(1, ranked)
            gated(FULL, 0, GATE[LAST:2 * LAST, :], None, LAST)
            mixed(FULL, 0, rows=LAST)
            low_a(FULL, 0, LAST)
            unit(1, 0, 0)
            unit(1, 1, 1)
            finish(0)
            with v.Fori(1, MIXED // 2) as j:
                unit(1, 2 * j, 0)
                unit(1, 2 * j + 1, 1)
            with v.Fori(MIXED // 2, FULL // 2 - 1) as j:
                unit(1, 2 * j, 0, own_mix=False)
                unit(1, 2 * j + 1, 1, own_mix=False)
            unit(1, FULL - 2, 0, own_mix=False)
            last_n = 2 * UNITS - 1
            gated(last_n - 1, 0, GATE_LAST[LAST:2 * LAST, :], None, LAST)
            mixed(last_n - 1, 0, rows=LAST)
            v.wait_ge(silu_done, last_n + 1)
            after(did(nc.vector.tensor_tensor(silu[:, 1, :], silu[:, 1, :], MIX[:], ALU.mult)))
            v.wait_ge(up_done, HALVES * FULL)
            nc.vector.tensor_tensor(act[:, 1, :], silu[:, 1, :], UP[:], ALU.mult).then_inc(act_done, 1)
            low_a(last_n - 1, 0, LAST)
            low_a(last_n, 1)
            finish(1)

        @block.tensor
        def _(pe):
            def ctx_block_max(h):
                pe.wait_ge(ctx_amax, h + 1)
                if h == 0:
                    pe.wait_ge(consts, 1)
                else:
                    pe.wait_ge(ex_in_ready, h)
                nc.tensor.transpose(BLK[h][0:CB, 0:P], amax_c[:, h, :], eye[:]).then_inc(ctx_amax_t, 1)

            def ctx_scale_rows(h):
                pe.wait_ge(ctx_diag, h + 1)
                nc.tensor.matmul(BLK[h][:, P:P + 2 * CB], ones[:], diag[:, h, :], start=True, stop=True).then_inc(ctx_scales, 1)

            def transpose_xq(b):
                pe.wait_ge(xq_ready, b + 1)
                if b == 2:
                    pe.wait_ge(ctx_scales_copied, 2)
                if b == 3:
                    pe.wait_ge(comb_ready, 1)
                view = qt_view(b)
                for jj, j in enumerate(tiles(b)):
                    for k in range(KC):
                        last = nc.tensor.transpose(view[:, k, jj * P:(jj + 1) * P], xq[:, j, k, :], eye_b[:])
                last.then_inc(xqt_psum, 1)

            def attend(b):
                pe.wait_ge(xqt_ready, b + 1)
                pe.wait_ge(cq_ready[b], 1)
                if b == 2:
                    pe.wait_ge(logits_copied, 1)
                if b == 3:
                    pe.wait_ge(x1_ready[b - 1], 1)
                for k in range(KC):
                    for jj in range(BT):
                        last = nc.tensor.matmul(ATT[b][k][:, jj * D:(jj + 1) * D], xqt[:, b, k, jj * P:(jj + 1) * P],
                                                cq[:, b, k, :], start=True, stop=True)
                last.then_inc(att_ready, 1)

            def transpose_tokens(b, src, dst, done):
                for k in range(KC):
                    for jj, j in enumerate(tiles(b)):
                        last = nc.tensor.transpose(dst[b][:, k * S + jj * P:k * S + (jj + 1) * P], src[:, j, k * P:(k + 1) * P], eye[:])
                last.then_inc(done, 1)

            def transpose_x1(b):
                pe.wait_ge(x1_ready[b], 1)
                transpose_tokens(b, x1, X1T, x1t_psum)

            def transpose_y2(b):
                pe.wait_ge(y2_ready, b + 1)
                if b == 2:
                    pe.wait_ge(x1t_copied, 3)
                transpose_tokens(b, y2, Y2T, y2t_psum)

            def router(h, i):
                ts = slice((HB * h + i) * S, (HB * h + i + 1) * S)
                pe.wait_ge(gate_split, 1)
                pe.wait_ge(h_lo_done, HB * h + i + 1)
                pe.wait_ge(x1t_copied, HB * (h + 1))
                last = three_passes(LOGIT[h][:, i * S:(i + 1) * S], [(gate_hi[:, k, :], gate_lo[:, k, :]) for k in range(KC)],
                                    [(h_hi[:, k, ts], h_lo[:, k, ts]) for k in range(KC)], True, True)
                if i == HB - 1:
                    last.then_inc(logits_ready, 1)

            def transpose_logits(h):
                pe.wait_ge(logits_copied, h + 1)
                for jj in range(HT):
                    last = nc.tensor.transpose(LOGIT_T[h][:, jj * GP:(jj + 1) * GP], lg_rows[:, jj * P:(jj + 1) * P],
                                               eye[0:GP, 0:GP])
                last.then_inc(logits_t, 1)

            def transpose_comb(h):
                pe.wait_ge(comb_split, h + 1)
                view = combt_view(h)
                for jj in range(HT):
                    last = nc.tensor.transpose(view[:, jj * P:(jj + 1) * P], comb_parts[:, jj, :], eye_b[:])
                last.then_inc(comb_psum, 1)

            def three_passes(out, w, x_of, start, stop):
                blocks = len(w)
                for k in range(blocks):
                    for i, (a, b) in enumerate(((0, 0), (0, 1), (1, 0))):
                        last = nc.tensor.matmul(out, w[k][a], x_of[k][b], start=(start and k == 0 and i == 0),
                                                stop=(stop and k == blocks - 1 and i == 2))
                return last

            def tokens(h):
                ts = slice(h * HN, (h + 1) * HN)
                return [(h_hi[:, k, ts], h_lo[:, k, ts]) for k in range(KC)]

            def w_gu(slot, which):
                at = which * KC * P
                return [(w_hi[:, slot, at + k * P:at + (k + 1) * P], w_lo[:, slot, at + k * P:at + (k + 1) * P])
                        for k in range(KC)]

            def keep_clock_up(count):
                for _ in range(count):
                    nc.tensor.matmul(UP[:], eye_b[:], xqt[:, 0].rearrange("p k t -> p (k t)"), start=True, stop=True)

            def gate(h, n, slot, bank=GATE):
                pe.wait_ge(gu_lo_done, n + 1)
                three_passes(bank[:], w_gu(slot, 0), tokens(h), True, True).then_inc(gate_done, 1)

            def gate_first_block(h, slot):
                three_passes(GATE[:], w_gu(slot, 0)[:1], tokens(h)[:1], True, False)

            def gate_other_block(h, slot):
                three_passes(GATE[:], w_gu(slot, 0)[1:], tokens(h)[1:], False, True).then_inc(gate_done, 1)

            def up(h, slot, bank=UP):
                three_passes(bank[:], w_gu(slot, 1), tokens(h), True, True).then_inc(up_done, 1)

            def mix(h, c, rows=P):
                nc.tensor.matmul(MIX[0:rows, :], spread[:, bass.ds(c * P, rows)], comb_t[:, h, :],
                                 start=True, stop=True).then_inc(mix_done, 1)

            def down(h, n, slot, start=False, stop=False, rows=P):
                pe.wait_ge(d_lo_done, n + 1)
                pe.wait_ge(a_lo_done, n + 1)
                for k in range(KC):
                    ks = slice(GU + k * P, GU + (k + 1) * P)
                    last = three_passes(OUT[h][k][:], [(w_hi[0:rows, slot, ks], w_lo[0:rows, slot, ks])],
                                        [(a_hi[0:rows, slot, :], a_lo[0:rows, slot, :])], start, stop)
                    if stop:
                        last.then_inc(half_done, 1)
                return last

            def products(h, c, s):
                n, slot = UNITS * h + c, (s + h) % 2
                pe.wait_ge(silu_done, n)
                gate(h, n, slot)
                pe.wait_ge(gated_done, n)
                up(h, slot)

            def mix_and_down(h, c, s, start=False):
                n, slot = UNITS * h + c, (s + h) % 2
                pe.wait_ge(act_done, n)
                mix(h, c)
                down(h, n - 1, 1 - slot, start)

            def shared_unit(h, c, s):
                products(h, c, s)
                down(h, UNITS * h + c - 1, 1 - (s + h) % 2)

            def unit(h, c, s):
                products(h, c, s)
                mix_and_down(h, c, s)

            ctx_block_max(0)
            ctx_scale_rows(0)
            transpose_xq(0)
            attend(0)
            transpose_xq(1)
            attend(1)
            keep_clock_up(9)
            transpose_x1(0)
            transpose_x1(1)
            transpose_y2(0)
            transpose_y2(1)
            for b in range(HB):
                router(0, b)
            pe.wait_ge(gu_lo_done, 1)
            gate_first_block(0, 0)
            transpose_logits(0)
            gate_other_block(0, 0)
            up(0, 0)
            gate(0, 1, 1, OUT[0][0])
            pe.wait_ge(ex_in_ready, 1)
            up(0, 1, OUT[0][1])
            transpose_comb(0)
            ctx_block_max(1)
            pe.wait_ge(gu_lo_done, 3)
            pe.wait_ge(silu_done, 1)
            gate_first_block(0, 0)
            pe.wait_ge(sel_landed, 16)
            pe.wait_ge(comb_ready, 1)
            mix(0, 0)
            gate_other_block(0, 0)
            pe.wait_ge(gated_done, 1)
            up(0, 0)
            pe.wait_ge(act_done, 1)
            mix(0, 1)
            pe.wait_ge(gated_done, 2)
            down(0, 0, 0, start=True)
            mix_and_down(0, 2, 0)
            ctx_scale_rows(1)
            for c in range(3, 7):
                unit(0, c, c % 2)
            transpose_xq(2)
            unit(0, 7, 1)
            products(0, 8, 0)
            transpose_xq(3)
            attend(2)
            mix_and_down(0, 8, 0)
            unit(0, 9, 1)
            products(0, 10, 0)
            attend(3)
            mix_and_down(0, 10, 0)
            transpose_x1(2)
            unit(0, 11, 1)
            transpose_y2(2)
            shared_unit(0, 12, 0)
            transpose_x1(3)
            products(0, 13, 1)
            transpose_y2(3)
            down(0, 12, 0)
            products(0, 14, 0)
            for b in range(HB):
                router(1, b)
            down(0, 13, 1)
            transpose_logits(1)
            shared_unit(0, 15, 1)
            pe.wait_ge(silu_done, FULL)
            gate(0, FULL, 0)
            down(0, FULL - 1, 1)
            gate(1, UNITS, 1, LOGIT[1])
            transpose_comb(1)
            pe.wait_ge(gated_done, UNITS - 1)
            up(1, 1)
            down(0, UNITS - 1, 0, stop=True, rows=LAST)
            pe.wait_ge(comb_ready, HALVES)
            mix(1, 0)
            products(1, 1, 1)
            mix_and_down(1, 1, 1, start=True)
            with pe.Fori(1, MIXED // 2) as j:
                unit(1, 2 * j, 0)
                unit(1, 2 * j + 1, 1)
            with pe.Fori(MIXED // 2, FULL // 2 - 1) as j:
                shared_unit(1, 2 * j, 0)
                shared_unit(1, 2 * j + 1, 1)
            shared_unit(1, FULL - 2, 0)
            last_n = 2 * UNITS - 1
            gate(1, last_n - 1, 0, GATE_LAST)
            pe.wait_ge(silu_done, last_n - 1)
            gate(1, last_n, 1)
            pe.wait_ge(gated_done, last_n - 1)
            up(1, 1)
            down(1, last_n - 2, 1).then_inc(down_slot_free, 1)
            down(1, last_n - 1, 0, rows=LAST)
            down(1, last_n, 1, stop=True)


def kernel(**inputs):
    import numpy as np
    import concourse.bacc as bacc
    from concourse.bass_utils import run_bass_kernel_spmd

    a = {k: np.asarray(v) for k, v in inputs.items()}
    xs = np.ascontiguousarray(a["x"].reshape(TILES, P, D).transpose(1, 0, 2))
    ctx_t = np.ascontiguousarray(a["ctx_2048"].reshape(B, D, KC, P).transpose(3, 0, 2, 1))
    gate = np.concatenate([a["L0_ffn_gate_w"], a["L0_ffn_shared_gate_w"], np.zeros((GP - G, D), np.float32)])
    gate_t = np.ascontiguousarray(gate.reshape(GP, KC, P).transpose(2, 1, 0))
    gw = np.concatenate([a["L0_ffn_wg"].reshape(E * EI, D), a["L0_ffn_swg"]])
    uw = np.concatenate([a["L0_ffn_wu"].reshape(E * EI, D), a["L0_ffn_swu"]])
    dw = np.concatenate([a["L0_ffn_wd"].transpose(0, 2, 1).reshape(E * EI, D), a["L0_ffn_swd"].T])

    def cols(w, chunks, rows):
        return w.reshape(chunks, rows, KC, P).transpose(0, 3, 2, 1).reshape(chunks, P, KC * rows)

    cut = FULL * P
    w_full = np.ascontiguousarray(np.concatenate(
        [cols(gw[:cut], FULL, P), cols(uw[:cut], FULL, P), dw[:cut].reshape(FULL, P, D)], axis=2))
    last_d = np.concatenate([dw[cut:], np.zeros((P - LAST, D), np.float32)])
    w_last = np.ascontiguousarray(np.concatenate(
        [cols(np.concatenate([gw[cut:], uw[cut:]]), 1, 2 * LAST)[0], last_d], axis=1))
    owner = np.concatenate([np.repeat(np.arange(E), EI), np.full(SI, E)])
    sel = np.ascontiguousarray(np.tile(np.eye(G, dtype=np.float16)[:, owner], (3, 1)))

    arrays = {"xs": xs, "ctx_t": ctx_t, "g_x": a["g_xattn"], "g_f": a["g_ffn"], "gate_t": gate_t,
              "w_full": w_full, "w_last": w_last, "sel": sel}
    nc = bacc.Bacc("TRN2", target_bir_lowering=False, num_devices=1)
    args = [nc.dram_tensor(n, v.shape, mybir.dt.from_np(v.dtype), kind="ExternalInput").ap() for n, v in arrays.items()]
    out_t = nc.dram_tensor("out_t", (KC, P, T), F32, kind="ExternalOutput").ap()
    flamingo_gated_block(nc, *args, out_t)
    r = run_bass_kernel_spmd(nc, [arrays], core_ids=[0])
    got = r.results[0]["out_t"]
    return np.ascontiguousarray(np.asarray(got).reshape(D, T).T).reshape(B, S, D)
```
